# Optimizing a Trainium2 kernel written in Bass

```python
import numpy as np
import jax
import jax.numpy as jnp

def _softmax(x, axis=-1):
    return jax.nn.softmax(x, axis=axis)

def _gelu(x):
    return jax.nn.gelu(x, approximate=True)

def _silu(x):
    return jax.nn.silu(x)

def _sigmoid(x):
    return jax.nn.sigmoid(x)

def _layernorm(x, axis=-1, eps=1e-05):
    m = jnp.mean(x, axis=axis, keepdims=True)
    v = jnp.var(x, axis=axis, keepdims=True)
    return (x - m) / jnp.sqrt(v + eps)

def _scatter_add(tgt, idx, src, axis=0):
    return tgt.at[idx].add(src)

def _segment_sum(src, seg, n):
    return jax.ops.segment_sum(src, seg, n)
kernel_name = 'mk_sandwich_d1_jaxref_r8_550461'

def setup_inputs(seed: int=0):
    np.random.seed(seed)
    _w = jnp.asarray

    def _L0_attn_setup():
        import jax, jax.numpy as jnp
        import numpy as np
        import math
        D_MODEL = 256
        D_STATE = 64
        D_CONV = 4
        EXPAND = 2
        HEADDIM = 128
        NGROUPS = 1
        CHUNK = 32
        D_INNER = EXPAND * D_MODEL
        NHEADS = D_INNER // HEADDIM
        CONV_DIM = D_INNER + 2 * NGROUPS * D_STATE
        D_IN_PROJ = 2 * D_INNER + 2 * NGROUPS * D_STATE + NHEADS
        BATCH, SEQLEN = (2, 512)
        EPS = 1e-05

        def segsum(x):
            T = x.shape[-1]
            xx = jnp.broadcast_to(x[..., :, None], x.shape + (T,))
            mask_lo = jnp.tril(jnp.ones((T, T), dtype=bool), -1)
            xx = jnp.where(mask_lo, xx, 0.0)
            s = jnp.cumsum(xx, axis=-2)
            mask = jnp.tril(jnp.ones((T, T), dtype=bool), 0)
            return jnp.where(mask, s, -jnp.inf)

        def ssd(X, A, B, C, block_len):
            b, L, h, p = X.shape
            c = L // block_len
            X = X.reshape(b, c, block_len, h, p)
            A = A.reshape(b, c, block_len, h).transpose(0, 3, 1, 2)
            B = B.reshape(b, c, block_len, h, -1)
            C = C.reshape(b, c, block_len, h, -1)
            A_cumsum = jnp.cumsum(A, axis=-1)
            Lmat = jnp.exp(segsum(A))
            Y_diag = jnp.einsum('bclhn,bcshn,bhcls,bcshp->bclhp', C, B, Lmat, X)
            decay_states = jnp.exp(A_cumsum[:, :, :, -1:] - A_cumsum)
            states = jnp.einsum('bclhn,bhcl,bclhp->bchpn', B, decay_states, X)
            init = jnp.zeros_like(states[:, :1])
            states = jnp.concatenate([init, states], axis=1)
            decay_chunk = jnp.exp(segsum(jnp.pad(A_cumsum[:, :, :, -1], ((0, 0), (0, 0), (1, 0)))))
            new_states = jnp.einsum('bhzc,bchpn->bzhpn', decay_chunk, states)
            states, final_state = (new_states[:, :-1], new_states[:, -1])
            Y_off = jnp.einsum('bclhn,bchpn,bhcl->bclhp', C, states, jnp.exp(A_cumsum))
            Y = (Y_diag + Y_off).reshape(b, L, h, p)
            return (Y, final_state)

        def causal_dwconv(x, w, b):
            C, K = w.shape
            y = jax.lax.conv_general_dilated(x.transpose(0, 2, 1), w[:, None, :], (1,), [(K - 1, 0)], feature_group_count=C)
            return y.transpose(0, 2, 1) + b
        key = jax.random.key(seed)
        ks = jax.random.split(key, 8)
        u = jax.random.normal(ks[0], (BATCH, SEQLEN, D_MODEL), dtype=jnp.float32)
        W_in = jax.random.normal(ks[1], (D_MODEL, D_IN_PROJ), dtype=jnp.float32) / np.sqrt(D_MODEL)
        conv_w = jax.random.normal(ks[2], (CONV_DIM, D_CONV), dtype=jnp.float32) / np.sqrt(D_CONV)
        conv_b = jnp.zeros((CONV_DIM,), dtype=jnp.float32)
        dt_min, dt_max, dt_floor = (0.001, 0.1, 0.0001)
        dt = jnp.exp(jax.random.uniform(ks[3], (NHEADS,)) * (math.log(dt_max) - math.log(dt_min)) + math.log(dt_min))
        dt = jnp.clip(dt, dt_floor)
        dt_bias = dt + jnp.log(-jnp.expm1(-dt))
        A_log = jnp.log(jax.random.uniform(ks[4], (NHEADS,), minval=1.0, maxval=16.0))
        D = jnp.ones((NHEADS,), dtype=jnp.float32)
        norm_w = jnp.ones((D_INNER,), dtype=jnp.float32)
        W_out = jax.random.normal(ks[5], (D_INNER, D_MODEL), dtype=jnp.float32) / np.sqrt(D_INNER)
        return {'u': u, 'W_in': W_in, 'conv_w': conv_w, 'conv_b': conv_b, 'dt_bias': dt_bias, 'A_log': A_log, 'D': D, 'norm_w': norm_w, 'W_out': W_out}
    _L0_attn_in = _L0_attn_setup()

    def _L0_ffn_setup():
        import jax, jax.numpy as jnp
        import numpy as np
        B, S, H = (2, 256, 256)
        E, K = (16, 4)
        I_MOE, I_SH = (176, 704)
        key = jax.random.key(seed)
        ks = jax.random.split(key, 9)

        def w(k, shape, fan_in):
            return jax.random.normal(k, shape, jnp.float32) * fan_in ** (-0.5)
        return {'hidden_states': jax.random.normal(ks[0], (B, S, H), jnp.float32), 'router_w': w(ks[1], (E, H), H), 'w_gate': w(ks[2], (E, H, I_MOE), H), 'w_up': w(ks[3], (E, H, I_MOE), H), 'w_down': w(ks[4], (E, I_MOE, H), I_MOE), 'sh_gate': w(ks[5], (H, I_SH), H), 'sh_up': w(ks[6], (H, I_SH), H), 'sh_down': w(ks[7], (I_SH, H), I_SH), 'sh_gate_w': w(ks[8], (H, 1), H)}
    _L0_ffn_in = _L0_ffn_setup()
    _d = {'L0_attn_u': _L0_attn_in['u'], 'L0_attn_W_in': _L0_attn_in['W_in'], 'L0_attn_conv_w': _L0_attn_in['conv_w'], 'L0_attn_conv_b': _L0_attn_in['conv_b'], 'L0_attn_dt_bias': _L0_attn_in['dt_bias'], 'L0_attn_A_log': _L0_attn_in['A_log'], 'L0_attn_D': _L0_attn_in['D'], 'L0_attn_norm_w': _L0_attn_in['norm_w'], 'L0_attn_W_out': _L0_attn_in['W_out'], 'L0_ffn_router_w': _L0_ffn_in['router_w'], 'L0_ffn_w_gate': _L0_ffn_in['w_gate'], 'L0_ffn_w_up': _L0_ffn_in['w_up'], 'L0_ffn_w_down': _L0_ffn_in['w_down'], 'L0_ffn_sh_gate': _L0_ffn_in['sh_gate'], 'L0_ffn_sh_up': _L0_ffn_in['sh_up'], 'L0_ffn_sh_down': _L0_ffn_in['sh_down'], 'L0_ffn_sh_gate_w': _L0_ffn_in['sh_gate_w']}
    _x0 = _d['L0_attn_u']
    _d['L0_attn_u'] = jax.random.normal(jax.random.fold_in(jax.random.key(seed), 1), (8, 512, 256), dtype=_x0.dtype)
    del _x0
    return _d

def reference(L0_attn_u, L0_attn_W_in, L0_attn_conv_w, L0_attn_conv_b, L0_attn_dt_bias, L0_attn_A_log, L0_attn_D, L0_attn_norm_w, L0_attn_W_out, L0_ffn_router_w, L0_ffn_w_gate, L0_ffn_w_up, L0_ffn_w_down, L0_ffn_sh_gate, L0_ffn_sh_up, L0_ffn_sh_down, L0_ffn_sh_gate_w):

    def _L0_attn_ref(u, W_in, conv_w, conv_b, dt_bias, A_log, D, norm_w, W_out):
        import jax, jax.numpy as jnp
        import numpy as np
        import math
        D_MODEL = 256
        D_STATE = 64
        D_CONV = 4
        EXPAND = 2
        HEADDIM = 128
        NGROUPS = 1
        CHUNK = 32
        D_INNER = EXPAND * D_MODEL
        NHEADS = D_INNER // HEADDIM
        CONV_DIM = D_INNER + 2 * NGROUPS * D_STATE
        D_IN_PROJ = 2 * D_INNER + 2 * NGROUPS * D_STATE + NHEADS
        BATCH, SEQLEN = (2, 512)
        EPS = 1e-05

        def segsum(x):
            T = x.shape[-1]
            xx = jnp.broadcast_to(x[..., :, None], x.shape + (T,))
            mask_lo = jnp.tril(jnp.ones((T, T), dtype=bool), -1)
            xx = jnp.where(mask_lo, xx, 0.0)
            s = jnp.cumsum(xx, axis=-2)
            mask = jnp.tril(jnp.ones((T, T), dtype=bool), 0)
            return jnp.where(mask, s, -jnp.inf)

        def ssd(X, A, B, C, block_len):
            b, L, h, p = X.shape
            c = L // block_len
            X = X.reshape(b, c, block_len, h, p)
            A = A.reshape(b, c, block_len, h).transpose(0, 3, 1, 2)
            B = B.reshape(b, c, block_len, h, -1)
            C = C.reshape(b, c, block_len, h, -1)
            A_cumsum = jnp.cumsum(A, axis=-1)
            Lmat = jnp.exp(segsum(A))
            Y_diag = jnp.einsum('bclhn,bcshn,bhcls,bcshp->bclhp', C, B, Lmat, X)
            decay_states = jnp.exp(A_cumsum[:, :, :, -1:] - A_cumsum)
            states = jnp.einsum('bclhn,bhcl,bclhp->bchpn', B, decay_states, X)
            init = jnp.zeros_like(states[:, :1])
            states = jnp.concatenate([init, states], axis=1)
            decay_chunk = jnp.exp(segsum(jnp.pad(A_cumsum[:, :, :, -1], ((0, 0), (0, 0), (1, 0)))))
            new_states = jnp.einsum('bhzc,bchpn->bzhpn', decay_chunk, states)
            states, final_state = (new_states[:, :-1], new_states[:, -1])
            Y_off = jnp.einsum('bclhn,bchpn,bhcl->bclhp', C, states, jnp.exp(A_cumsum))
            Y = (Y_diag + Y_off).reshape(b, L, h, p)
            return (Y, final_state)

        def causal_dwconv(x, w, b):
            C, K = w.shape
            y = jax.lax.conv_general_dilated(x.transpose(0, 2, 1), w[:, None, :], (1,), [(K - 1, 0)], feature_group_count=C)
            return y.transpose(0, 2, 1) + b
        batch, seqlen, _ = u.shape
        zxbcdt = u @ W_in
        z, xBC, dt = jnp.split(zxbcdt, [D_INNER, D_INNER + CONV_DIM], axis=-1)
        dt = jax.nn.softplus(dt + dt_bias)
        xBC = jax.nn.silu(causal_dwconv(xBC, conv_w, conv_b))
        x, B, C = jnp.split(xBC, [D_INNER, D_INNER + NGROUPS * D_STATE], axis=-1)
        x = x.reshape(batch, seqlen, NHEADS, HEADDIM)
        B = jnp.broadcast_to(B.reshape(batch, seqlen, NGROUPS, D_STATE), (batch, seqlen, NHEADS, D_STATE))
        C = jnp.broadcast_to(C.reshape(batch, seqlen, NGROUPS, D_STATE), (batch, seqlen, NHEADS, D_STATE))
        A = -jnp.exp(A_log)
        x_scaled = x * dt[..., None]
        A_dt = A * dt
        y, _final = ssd(x_scaled, A_dt, B, C, CHUNK)
        y = y.reshape(batch, seqlen, D_INNER)
        x_flat = x.reshape(batch, seqlen, D_INNER)
        D_full = jnp.repeat(D, HEADDIM)
        y = y + x_flat * D_full
        yg = y * jax.nn.silu(z)
        var = jnp.mean(yg * yg, axis=-1, keepdims=True)
        y = yg * jax.lax.rsqrt(var + EPS) * norm_w
        return y @ W_out

    def _L0_ffn_ref(hidden_states, router_w, w_gate, w_up, w_down, sh_gate, sh_up, sh_down, sh_gate_w):
        import jax, jax.numpy as jnp
        import numpy as np
        B, S, H = (2, 256, 256)
        E, K = (16, 4)
        I_MOE, I_SH = (176, 704)
        orig = hidden_states.shape
        h = hidden_states.reshape(-1, orig[-1])
        N = h.shape[0]
        logits = h @ router_w.T
        probs = jax.nn.softmax(logits.astype(jnp.float32), axis=-1)
        top_vals, top_idx = jax.lax.top_k(probs, K)
        top_vals = top_vals / jnp.maximum(top_vals.sum(-1, keepdims=True), 1e-09)
        top_vals = top_vals.astype(h.dtype)
        comb = jnp.zeros((N, E), h.dtype).at[jnp.arange(N)[:, None], top_idx].add(top_vals)
        g = jnp.einsum('nh,ehi->eni', h, w_gate)
        u = jnp.einsum('nh,ehi->eni', h, w_up)
        y = jnp.einsum('eni,eih->enh', jax.nn.silu(g) * u, w_down)
        routed = jnp.einsum('enh,ne->nh', y, comb)
        shared = jax.nn.silu(h @ sh_gate) * (h @ sh_up) @ sh_down
        sg = jax.nn.sigmoid(h @ sh_gate_w)
        return (routed + sg * shared).reshape(orig)
    x = L0_attn_u
    x = x + _layernorm(_L0_attn_ref(_layernorm(x, axis=-1), L0_attn_W_in, L0_attn_conv_w, L0_attn_conv_b, L0_attn_dt_bias, L0_attn_A_log, L0_attn_D, L0_attn_norm_w, L0_attn_W_out), axis=-1)
    x = x + _layernorm(_L0_ffn_ref(_layernorm(x, axis=-1), L0_ffn_router_w, L0_ffn_w_gate, L0_ffn_w_up, L0_ffn_w_down, L0_ffn_sh_gate, L0_ffn_sh_up, L0_ffn_sh_down, L0_ffn_sh_gate_w), axis=-1)
    return x

_drawn_inputs = setup_inputs


def setup_inputs(seed=0):
    import zlib

    import numpy as np

    out = dict(_drawn_inputs(seed))
    spreads = {'L0_attn_conv_b': (0.0, 0.1), 'L0_attn_D': (1.0, 0.2), 'L0_attn_norm_w': (1.0, 0.2)}
    factors = {}
    for name, (base, spread) in spreads.items():
        noise = np.random.default_rng([zlib.crc32(name.encode()), seed]).standard_normal(out[name].shape)
        drawn = base * np.exp(spread * noise) if base else spread * noise
        out[name] = jnp.asarray(drawn.astype(out[name].dtype))
    for name, factor in factors.items():
        out[name] = (out[name] * factor).astype(out[name].dtype)
    return out
```

```python
import numpy as np
import concourse.bass as bass
from concourse import mybir
from contextlib import ExitStack

BATCH, SEQ, D_MODEL = 8, 512, 256
TOKENS = BATCH * SEQ
HEADS, HEAD_DIM, STATE = 4, 128, 64
D_INNER = HEADS * HEAD_DIM
TAPS = 4
EXPERTS, TOP_K, I_MOE, I_SHARED = 16, 4, 176, 704
LN_EPS = 1e-5

P = 128
KD = D_MODEL // P
CHUNK = 128
QS = SEQ // CHUNK
TILES = TOKENS // P
GATES = EXPERTS + 1
PARTS = 3
XBC_TILES = (D_INNER + 2 * STATE) // P
W_IN_COLS = 2 * D_INNER + 2 * STATE + HEADS
DT_COL = W_IN_COLS - HEADS
ROUTED_CHUNKS = EXPERTS * I_MOE // P
SHARED_CHUNKS = -(-I_SHARED // P)
CHUNKS = ROUTED_CHUNKS + SHARED_CHUNKS
GROUP = 2
GROUPS = CHUNKS // GROUP
W_COLS = KD * P * 2 + D_MODEL
G_OFF, U_OFF, D_OFF = 0, KD * P, 2 * KD * P


def sandwich_kernel(nc, u, w_in, w_out, small_d,
                    gates_w, moe_w, ident_d, causal_d, later_d, index_d, spread_d, out):
    F32, F32R, BF16, U32 = mybir.dt.float32, mybir.dt.float32r, mybir.dt.bfloat16, mybir.dt.uint32
    ALU, ACT, AX = mybir.AluOpType, mybir.ActivationFunctionType, mybir.AxisListType

    whole = ExitStack()
    sems = {}

    def sem(name):
        if name not in sems:
            sems[name] = whole.enter_context(nc.semaphore(name))
        return sems[name]

    def hold(engine):
        engine.sem_inc(sem("held"), 1)

    def f32(ap):
        return ap.bitcast(F32)

    with whole:
        x1_dram = nc.dram_tensor("x1_scratch", (TILES, P, D_MODEL), F32, kind="Internal").ap()

        def alloc(stack, name, shape, dt=F32):
            return stack.enter_context(nc.sbuf_tensor(name, shape, dt))

        xt_hi = alloc(whole, "xt_hi", [P, KD, TOKENS], F32R)
        xt_lo = alloc(whole, "xt_lo", [P, KD, TOKENS], F32R)
        ident = alloc(whole, "ident", [P, P])
        exponent = alloc(whole, "exponent", [P, QS])
        rw_hi = alloc(whole, "rw_hi", [P, KD, GATES], F32R)
        rw_lo = alloc(whole, "rw_lo", [P, KD, GATES], F32R)

        with ExitStack() as st:
            win_hi = alloc(st, "win_hi", [P, KD, W_IN_COLS], F32R)
            win_lo = alloc(st, "win_lo", [P, KD, W_IN_COLS], F32R)
            wo_hi = alloc(st, "wo_hi", [P, HEADS, D_MODEL], F32R)
            wo_lo = alloc(st, "wo_lo", [P, HEADS, D_MODEL], F32R)
            rw_raw = alloc(st, "rw_raw", [P, KD, GATES])
            causal = alloc(st, "causal", [P, P])
            later = alloc(st, "later", [P, P + STATE])
            ones = alloc(st, "ones", [P, P])
            small = alloc(st, "small", [P, XBC_TILES * (TAPS + 1) + 4 * HEADS])
            conv_taps = small[:, 0:XBC_TILES * TAPS].rearrange("p (m k) -> p m k", k=TAPS)
            after = XBC_TILES * TAPS
            conv_bias = small[:, after:after + XBC_TILES]
            after += XBC_TILES
            norm_col, dtb_row, alog_row, d_row = (
                small[:, after + i * HEADS:after + (i + 1) * HEADS] for i in range(4))
            aneg_row = alloc(st, "aneg_row", [P, HEADS])
            xbc = [alloc(st, f"xbc{i}", [P, XBC_TILES, SEQ]) for i in range(2)]
            c_act = [alloc(st, f"c_act{i}", [STATE, SEQ]) for i in range(2)]
            gate_z = [alloc(st, f"gate_z{i}", [P, HEADS, SEQ]) for i in range(2)]
            conv_in = [alloc(st, f"conv_in{i}", [P, TAPS - 1 + SEQ]) for i in range(2)]
            conv_acc = [alloc(st, f"conv_acc{i}", [P, SEQ]) for i in range(2)]
            dt_rows = alloc(st, "dt_rows", [HEADS, SEQ])
            dt_y = alloc(st, "dt_y", [P, QS * HEADS])
            dt_neg = alloc(st, "dt_neg", [P, QS * HEADS])
            dt_nabs = alloc(st, "dt_nabs", [P, QS * HEADS])
            dt_e = alloc(st, "dt_e", [P, QS * HEADS])
            dt_l = alloc(st, "dt_l", [P, QS * HEADS])
            dt = [alloc(st, f"dt{i}", [P, QS * HEADS]) for i in range(2)]
            a_dt = [alloc(st, f"a_dt{i}", [P, QS * HEADS]) for i in range(2)]
            carry = [alloc(st, f"carry{i}", [STATE, QS * HEADS]) for i in range(2)]
            x_in = alloc(st, "x_in", [P, QS, D_MODEL])
            x_norm = alloc(st, "x_norm", [P, QS, D_MODEL])
            st0 = alloc(st, "st0", [P, QS, 6])
            mv0 = alloc(st, "mv0", [P, QS, 2])
            ve0 = alloc(st, "ve0", [P, QS])
            rs0 = alloc(st, "rs0", [P, QS])
            am = [alloc(st, f"am{i}", [P, HEADS, P + STATE]) for i in range(2)]
            decay = [alloc(st, f"decay{i}", [P, HEADS, P]) for i in range(2)]
            mix = [alloc(st, f"mix{i}", [P, HEADS, P]) for i in range(2)]
            xs = [alloc(st, f"xs{i}", [P, HEADS, P]) for i in range(2)]
            xw = alloc(st, "xw", [P, HEADS, P])
            cb = [alloc(st, f"cb{i}", [P, P]) for i in range(2)]
            ce = [alloc(st, f"ce{i}", [STATE, HEADS, P]) for i in range(2)]
            ce_c = [alloc(st, f"ce_c{i}", [STATE, HEADS, P]) for i in range(2)]
            b_tok = [alloc(st, f"b_tok{i}", [P, STATE]) for i in range(2)]
            state = alloc(st, "state", [STATE, HEADS, P])
            state_dec = alloc(st, "state_dec", [STATE, HEADS, P])
            y_sum = alloc(st, "y_sum", [P, HEADS, P])
            yg = alloc(st, "yg", [P, HEADS, P])
            yg_hi = [alloc(st, f"yg_hi{i}", [P, HEADS, P], F32R) for i in range(2)]
            yg_lo = [alloc(st, f"yg_lo{i}", [P, HEADS, P], F32R) for i in range(2)]
            ysq = alloc(st, "ysq", [P, HEADS, P])
            x_res = [alloc(st, f"x_res{i}", [P, D_MODEL]) for i in range(2)]
            shifted = alloc(st, "shifted", [P, D_MODEL])
            x1 = [alloc(st, f"x1_{i}", [P, D_MODEL]) for i in range(2)]
            xn2 = alloc(st, "xn2", [P, D_MODEL])
            st1 = alloc(st, "st1", [P, 6]); mv1 = alloc(st, "mv1", [P, 2])
            sse = alloc(st, "sse", [P, 1]); ve1 = alloc(st, "ve1", [P, 1]); rs1 = alloc(st, "rs1", [P, 1])
            st2 = alloc(st, "st2", [P, 6]); mv2 = alloc(st, "mv2", [P, 2])
            ve2 = alloc(st, "ve2", [P, 1]); rs2 = alloc(st, "rs2", [P, 1])
            win_raw = xbc[1][:].rearrange("p a b -> p (a b)")[:, 0:KD * W_IN_COLS].rearrange(
                "p (k n) -> p k n", k=KD)
            wo_raw = gate_z[1][:].rearrange("p a b -> p (a b)")[:, 0:HEADS * D_MODEL].rearrange(
                "p (k n) -> p k n", k=HEADS)

            wo_scaled = gate_z[1][:].rearrange("p a b -> p (a b)")[:, HEADS * D_MODEL:2 * HEADS * D_MODEL].rearrange(
                "p (k n) -> p k n", k=HEADS)

            def bank(name, dt=F32):
                return st.enter_context(nc.psum_tensor(name, [P, 512], dt))

            pa = [bank("pa0"), bank("pa1")]
            p_seg, p_cum, p_y, p_state, p_xt, p_misc = (
                bank(n) for n in ("p_seg", "p_cum", "p_y", "p_state", "p_xt", "p_misc"))
            CB, BT = slice(0, P), slice(P, P + STATE)
            DTT, TOT = slice(192, 192 + QS * HEADS), slice(224, 224 + QS * HEADS)

            ORDER = ["s", "p", "a0", "a1", "b0", "v0", "a2", "r0", "b1", "n0", "v1", "a3", "r1", "t0",
                     "b2", "n1", "v2", "b3", "la", "r2", "t1", "n2", "lb", "lc", "v3", "r3", "t2",
                     "n3", "t3"]

            def use_s(b, n):
                return n // 2 + 3 if isinstance(b, int) and b == 0 else b * 10 - 2 + n // 2

            def after_s(b):
                return 76 if isinstance(b, int) and b == BATCH - 1 else b * 10 + 12

            def use_v(b, q):
                return after_s(b) + q + 1 + (q == 3 and not (isinstance(b, int) and b >= BATCH - 2))

            def use_t(b, q):
                return after_s(b) + q + 1 + (q >= 2 and not (isinstance(b, int) and b >= BATCH - 2))

            def use_l(b, k):
                return b + 1 if isinstance(b, int) and b < 2 else b * 10 - 4 - k

            def before(b, q):
                return b * QS + max(q - 1, 0)

            def walk(stages, loop):
                for b in range(2):
                    for s in ("la", "lb", "lc"):
                        stages[s](b)
                stages["s"](0, 0)
                stages["p"](0, 0)

                def pair(p, last):
                    for par in range(2):
                        b = p * 2 + par
                        for s in ORDER:
                            if s[0] == "l":
                                if not last:
                                    stages[s](b + 2)
                            elif s in "sp":
                                if not (last and par == 1):
                                    stages[s](b + 1, 1 - par)
                            else:
                                stages[s[0]](b, par, int(s[1]))

                with loop(0, BATCH // 2 - 1) as p:
                    pair(p, False)
                pair(BATCH // 2 - 1, True)

            nothing = {s: (lambda *a: None) for s in ("la", "lb", "lc", "s", "p", "a", "b", "v", "r", "n", "t")}
            TILE_ORDER = [("dt", 0)]
            for m in range(HEADS):
                TILE_ORDER += [("z", m), ("x", m)]
            TILE_ORDER.append(("x", HEADS))
            NT = len(TILE_ORDER)

            with nc.Block() as block:
                @block.sync
                def _(sp):
                    sp.dma_start(win_raw, w_in.rearrange("(k p) n -> p k n", p=P)).then_inc(sem("win_loaded"), 16)

                    def x_load(b):
                        sp.wait_ge(sem("x_normed"), b)
                        sp.dma_start(x_in[:], u_tiles(b)).then_inc(sem("x_loaded"), 16)

                    u4 = u.rearrange("b (q p) d -> b p q d", p=P)

                    def u_tiles(b):
                        return u4[b] if isinstance(b, int) else u4[bass.ds(b, 1)].rearrange("a p q d -> (a p) q d")

                    consts = [(ident[:], ident_d), (causal[:], causal_d), (later[:], later_d),
                             (small[:], small_d),
                             (rw_raw[:], gates_w.rearrange("(k p) e -> p k e", p=P))]
                    x_load(0)
                    for dst, src in consts:
                        sp.dma_start(dst, src).then_inc(sem("consts_loaded"), 16)
                    sp.dma_start(wo_raw, w_out.rearrange("(h p) n -> p h n", p=P)).then_inc(sem("wo_loaded"), 16)

                    x_tiles = u.rearrange("b (q p) d -> (b q) p d", p=P)

                    def tile_of(ap, j):
                        return ap[j] if isinstance(j, int) else ap[bass.ds(j, 1)].rearrange("a p d -> (a p) d")

                    def v(b, par, q):
                        j = b * QS + q
                        sp.wait_ge(sem(f"x1_done{q % 2}"), b * 2 + q // 2)
                        sp.dma_start(x_res[q % 2][:], tile_of(x_tiles, j)).then_inc(sem(f"res_loaded{q % 2}"), 16)

                    def r(b, par, q):
                        j = b * QS + q
                        sp.wait_ge(sem(f"x1_done{q % 2}"), b * 2 + q // 2 + 1)
                        sp.dma_start(tile_of(x1_dram, j), x1[q % 2][:]).then_inc(sem(f"x1_stored{q % 2}"), 16)

                    def la(b):
                        if isinstance(b, int) and b == 0:
                            return
                        x_load(b)

                    walk({**nothing, "la": la, "v": v, "r": r}, sp.Fori)
                    for i in range(2):
                        sp.wait_ge(sem(f"x1_stored{i}"), 16 * TILES // 2)

                @block.gpsimd
                def _(pool):
                    nc.gpsimd.memset(exponent[:], -0.5)
                    nc.gpsimd.memset(ones[:], 1.0).then_inc(sem("pool_consts"), 1)
                    pool.wait_ge(sem("pool_consts"), 1)

                    def la(b):
                        pool.wait_ge(sem("ve0_done"), b + 1)
                        nc.gpsimd.tensor_tensor(rs0[:], ve0[:], exponent[:], ALU.pow).then_inc(sem("rs0_done"), 1)

                    def a(b, par, q):
                        j, c = b * QS + q, q % 2
                        if q:
                            pool.wait_ge(sem("ce_done"), j + 1)
                            pool.wait_ge(sem("y_filled"), before(b, q))
                            nc.gpsimd.tensor_tensor(ce_c[c][:], ce[c][:], c_act[par][:, q * P:(q + 1) * P].unsqueeze(1).to_broadcast([STATE, HEADS, P]), ALU.mult).then_inc(sem("ce_c_done"), 1)
                        if q < QS - 1:
                            pool.wait_ge(sem("xs_done"), j + 1)
                            pool.wait_ge(sem("decay_done"), j + 1)
                            pool.wait_ge(sem("state_filled"), b * 3 + q)
                            nc.gpsimd.tensor_tensor(xw[:], xs[c][:], decay[c][:, :, P - 1:P].to_broadcast([P, HEADS, P]), ALU.mult).then_inc(sem("xw_done"), 1)

                    def bb(b, par, q):
                        j, c = b * QS + q, q % 2
                        if 0 < q < QS - 1:
                            pool.wait_ge(sem("state_done"), b * 3 + q)
                            pool.wait_ge(sem("carry_done"), b + 1)
                            nc.gpsimd.tensor_tensor(state_dec[:], state[:], carry[par][:, q * HEADS:(q + 1) * HEADS].unsqueeze(2).to_broadcast([STATE, HEADS, P]), ALU.mult).then_inc(sem("state_dec_done"), 1)
                        pool.wait_ge(sem("yg_hi_done"), j + 1)
                        pool.wait_ge(sem("yg_done"), j + 1)
                        pool.wait_ge(sem("v_filled"), before(b, q))
                        nc.gpsimd.tensor_tensor(yg_lo[c][:], yg[:], f32(yg_hi[c][:]), ALU.subtract).then_inc(sem("yg_lo_done"), 1)

                    def v(b, par, q):
                        pool.wait_ge(sem("ve1_done"), b * QS + q + 1)
                        nc.gpsimd.tensor_tensor(rs1[:], ve1[:], exponent[:, 0:1], ALU.pow).then_inc(sem("rs1_done"), 1)

                    def r(b, par, q):
                        pool.wait_ge(sem("ve2_done"), b * QS + q + 1)
                        nc.gpsimd.tensor_tensor(rs2[:], ve2[:], exponent[:, 0:1], ALU.pow).then_inc(sem("rs2_done"), 1)

                    walk({**nothing, "la": la, "a": a, "b": bb, "v": v, "r": r}, pool.Fori)

                @block.scalar
                def _(act):
                    act.wait_ge(sem("consts_loaded"), 16 * 5)
                    act.wait_ge(sem("win_loaded"), 16)
                    nc.scalar.activation(win_hi[:], win_raw, ACT.Copy).then_inc(sem("win_hi_done"), 1)
                    nc.scalar.activation(rw_hi[:], rw_raw[:], ACT.Copy).then_inc(sem("rw_hi_done"), 1)
                    nc.scalar.activation(aneg_row[:], alog_row, ACT.Exp).then_inc(sem("a_exp"), 1)
                    act.wait_ge(sem("wo_loaded"), 16)
                    for h in range(HEADS):
                        last = nc.scalar.activation(wo_scaled[:, h, :], wo_raw[:, h, :], ACT.Copy, scale=norm_col[:, h:h + 1])
                    last.then_inc(sem("wo_scaled_done"), 1)
                    act.wait_ge(sem("wo_scaled_done"), 1)
                    nc.scalar.activation(wo_hi[:], wo_scaled, ACT.Copy).then_inc(sem("wo_hi_done"), 1)

                    def lc(b):
                        for k in range(KD):
                            act.wait_ge(sem("xt_filled"), b * 2 + k + 1)
                            nc.scalar.activation(xt_hi[:, k, bass.ds(b * SEQ, SEQ)], pa[k][:], ACT.Copy).then_inc(sem("xt_hi_done"), 1)

                    def s(b, par):
                        waiting = []

                        def silu(m):
                            act.wait_ge(sem("conv_done"), b * XBC_TILES + m + 1)
                            src = conv_acc[m % 2]
                            if m < HEADS:
                                nc.scalar.activation(xbc[par][:, m, :], src[:], ACT.Silu).then_inc(sem("silu_done"), 1)
                            else:
                                nc.scalar.activation(xbc[par][0:STATE, m, :], src[0:STATE, :], ACT.Silu)
                                nc.scalar.activation(c_act[par][:], src[STATE:P, :], ACT.Silu).then_inc(sem("silu_done"), 1)

                        if not isinstance(b, int) or b > 1:
                            act.wait_ge(sem("y_filled"), (b - 1) * QS)
                            act.wait_ge(sem("yg_done"), (b - 1) * QS)
                        else:
                            act.wait_ge(sem("wo_lo_done"), 1)
                            act.wait_ge(sem("win_lo_done"), 1)
                        for n, (kind, m) in enumerate(TILE_ORDER):
                            act.wait_ge(sem("proj_filled"), b * NT + n + 1)
                            src = pa[n % 2]
                            free = sem(f"pa{n % 2}_free")
                            if kind == "dt":
                                if not (isinstance(b, int) and b == 0):
                                    act.wait_ge(sem("dtt_filled"), b)
                                nc.scalar.activation(dt_rows[:], src[0:HEADS, :], ACT.Copy).then_inc(free, 1)
                            elif kind == "z":
                                nc.scalar.activation(gate_z[par][:, m, :], src[:], ACT.Silu).then_inc(free, 1)
                            else:
                                act.wait_ge(sem("conv_done"), b * XBC_TILES + max(m - 1, 0))
                                if isinstance(b, int) and b == 0 and m < 2:
                                    act.wait_ge(sem("pads_zero"), 1)
                                nc.scalar.activation(conv_in[m % 2][:, TAPS - 1:], src[:], ACT.Copy).then_inc(sem("conv_in_done"), 1)
                                act.wait_ge(sem("silu_done"), b * XBC_TILES + max(m - 1, 0))
                                nc.scalar.activation(conv_acc[m % 2][:], src[:], ACT.Identity, bias=conv_bias[:, m:m + 1], scale=conv_taps[:, m, TAPS - 1:TAPS]).then_inc(free, 1)
                                waiting.append(m)
                                if len(waiting) > 1:
                                    silu(waiting.pop(0))
                        for m in waiting:
                            silu(m)

                    def p(b, par):
                        act.wait_ge(sem("dt_nabs_done"), b + 1)
                        nc.scalar.activation(dt_e[:], dt_nabs[:], ACT.Exp).then_inc(sem("dt_e_done"), 1)
                        act.wait_ge(sem("dt_e_done"), b + 1)
                        nc.scalar.activation(dt_l[:], dt_e[:], ACT.Ln, bias=1.0).then_inc(sem("dt_l_done"), 1)

                    def a(b, par, q):
                        j, c = b * QS + q, q % 2
                        act.wait_ge(sem("a_dt_done"), b + 1)
                        act.wait_ge(sem("seg_filled"), before(b, q))
                        for h in range(HEADS):
                            last = nc.scalar.activation(am[c][:, h, :], later[:], ACT.Copy, scale=a_dt[par][:, q * HEADS + h:q * HEADS + h + 1])
                        last.then_inc(sem("am_done"), 1)
                        if q == 0:
                            act.wait_ge(sem("tot_filled"), b + 1)
                            act.wait_ge(sem("state_dec_done"), b * 2)
                            nc.scalar.activation(carry[par][:], p_misc[0:STATE, TOT], ACT.Exp).then_inc(sem("carry_done"), 1)
                        act.wait_ge(sem("cb_done"), j + 1)
                        act.wait_ge(sem("state_filled"), b * 3 + (0, 0, 1, 2)[q])
                        nc.scalar.activation(b_tok[c][:], p_misc[:, BT], ACT.Copy).then_inc(sem("b_tok_done"), 1)
                        act.wait_ge(sem("xt_tok_filled"), j + 1)
                        act.wait_ge(sem("y_filled"), before(b, q))
                        act.wait_ge(sem("xw_done"), b * 3 + (0, 0, 1, 2)[q])
                        for h in range(HEADS):
                            last = nc.scalar.activation(xs[c][:, h, :], p_xt[:, h * P:(h + 1) * P], ACT.Copy, scale=dt[par][:, q * HEADS + h:q * HEADS + h + 1])
                        last.then_inc(sem("xs_done"), 1)
                        act.wait_ge(sem("seg_filled"), j + 1)
                        act.wait_ge(sem("mix_done"), before(b, q))
                        nc.scalar.activation(decay[c][:].rearrange("p h l -> p (h l)"), p_seg[:], ACT.Exp).then_inc(sem("decay_done"), 1)
                        act.wait_ge(sem("ce_c_done"), b * 3 + (0, 0, 0, 1)[q])
                        nc.scalar.activation(ce[c][:].rearrange("p h l -> p (h l)"), p_cum[0:STATE, :], ACT.Exp).then_inc(sem("ce_done"), 1)

                    def bb(b, par, q):
                        j, c = b * QS + q, q % 2
                        act.wait_ge(sem("yg_done"), j + 1)
                        act.wait_ge(sem("v_filled"), before(b, q))
                        act.wait_ge(sem("yg_lo_done"), before(b, q))
                        nc.scalar.activation(yg_hi[c][:], yg[:], ACT.Copy).then_inc(sem("yg_hi_done"), 1)
                        act.wait_ge(sem("v_filled"), j)
                        nc.scalar.activation(ysq[:], yg[:], ACT.Square).then_inc(sem("ysq_done"), 1)

                    def t(b, par, q):
                        j = b * QS + q
                        act.wait_ge(sem("t2_filled"), j + 1)
                        nc.scalar.activation(xt_hi[:, :, bass.ds(j * P, P)], pa[1][:, 0:KD * P].rearrange("p (k n) -> p k n", k=KD), ACT.Copy).then_inc(sem("t2_hi_done"), 1)

                    walk({**nothing, "lc": lc, "s": s, "p": p, "a": a, "b": bb, "t": t}, act.Fori)

                @block.vector
                def _(dve):
                    for i in range(2):
                        last = nc.vector.memset(conv_in[i][:, 0:TAPS - 1], 0.0)
                    last.then_inc(sem("pads_zero"), 1)

                    def setup():
                        dve.wait_ge(sem("win_hi_done"), 1)
                        nc.vector.tensor_tensor(win_lo[:], win_raw, f32(win_hi[:]), ALU.subtract).then_inc(sem("win_lo_done"), 1)
                        dve.wait_ge(sem("rw_hi_done"), 1)
                        nc.vector.tensor_tensor(rw_lo[:], rw_raw[:], f32(rw_hi[:]), ALU.subtract).then_inc(sem("rw_lo_done"), 1)
                        dve.wait_ge(sem("a_exp"), 1)
                        nc.vector.tensor_scalar(aneg_row[:], aneg_row[:], -1.0, None, ALU.mult).then_inc(sem("a_neg"), 1)
                        dve.wait_ge(sem("wo_hi_done"), 1)
                        nc.vector.tensor_tensor(wo_lo[:], wo_scaled, f32(wo_hi[:]), ALU.subtract).then_inc(sem("wo_lo_done"), 1)

                    def la(b):
                        dve.wait_ge(sem("x_loaded"), b * 16 + 16)
                        for q in range(QS):
                            last = nc.vector.bn_stats(st0[:, q, :], x_in[:, q, :])
                        last.then_inc(sem("st0_done"), 1)
                        dve.wait_ge(sem("st0_done"), b + 1)
                        hold(dve)
                        for q in range(QS):
                            last = nc.vector.bn_aggr(mv0[:, q, :], st0[:, q, :])
                        last.then_inc(sem("mv0_done"), 1)
                        dve.wait_ge(sem("mv0_done"), b + 1)
                        nc.vector.tensor_scalar(ve0[:].unsqueeze(2), mv0[:, :, 1:2], LN_EPS, None, ALU.add).then_inc(sem("ve0_done"), 1)

                    def lb(b):
                        dve.wait_ge(sem("rs0_done"), b + 1)
                        dve.wait_ge(sem("xt_filled"), b * 2)
                        for q in range(QS):
                            last = nc.vector.tensor_scalar(x_norm[:, q, :], x_in[:, q, :], mv0[:, q, 0:1], rs0[:, q:q + 1], ALU.subtract, ALU.mult)
                        last.then_inc(sem("x_normed"), 1)

                    def lc(b):
                        for k in range(KD):
                            dve.wait_ge(sem("xt_hi_done"), b * 2 + k + 1)
                            part = bass.ds(b * SEQ, SEQ)
                            nc.vector.tensor_tensor(xt_lo[:, k, part], pa[k][:], f32(xt_hi[:, k, part]), ALU.subtract).then_inc(sem(f"pa{k}_free"), 1)
                        if isinstance(b, int) and b == 1:
                            setup()

                    def s(b, par):
                        for m in range(XBC_TILES):
                            dve.wait_ge(sem("conv_in_done"), b * XBC_TILES + m + 1)
                            slot = TILE_ORDER.index(("x", m))
                            dve.wait_ge(sem(f"pa{slot % 2}_free"), use_s(b, slot))
                            for k in range(TAPS - 1):
                                last = nc.vector.scalar_tensor_tensor(conv_acc[m % 2][:], conv_in[m % 2][:, k:k + SEQ], conv_taps[:, m, k:k + 1], conv_acc[m % 2][:], ALU.mult, ALU.add)
                                if k < TAPS - 2:
                                    last.then_inc(sem("tap_done"), 1)
                                    dve.wait_ge(sem("tap_done"), (b * XBC_TILES + m) * (TAPS - 2) + k + 1)
                            last.then_inc(sem("conv_done"), 1)
                        dve.wait_ge(sem("dtt_filled"), b + 1)
                        nc.vector.tensor_tensor(dt_y[:].rearrange("p (q h) -> p q h", h=HEADS), p_misc[:, DTT].rearrange("p (q h) -> p q h", h=HEADS), dtb_row.unsqueeze(1).to_broadcast([P, QS, HEADS]), ALU.add).then_inc(sem("dt_y_done"), 1)
                        dve.wait_ge(sem("dt_y_done"), b + 1)
                        nc.vector.tensor_scalar(dt_neg[:], dt_y[:], -1.0, None, ALU.mult).then_inc(sem("dt_neg_done"), 1)
                        dve.wait_ge(sem("dt_neg_done"), b + 1)
                        nc.vector.tensor_tensor(dt_nabs[:], dt_y[:], dt_neg[:], ALU.min).then_inc(sem("dt_nabs_done"), 1)

                    def p(b, par):
                        dve.wait_ge(sem("dt_l_done"), b + 1)
                        nc.vector.scalar_tensor_tensor(dt[par][:], dt_y[:], 0.0, dt_l[:], ALU.max, ALU.add).then_inc(sem("dt_done"), 1)
                        dve.wait_ge(sem("dt_done"), b + 1)
                        nc.vector.tensor_tensor(a_dt[par][:].rearrange("p (q h) -> p q h", h=HEADS), dt[par][:].rearrange("p (q h) -> p q h", h=HEADS), aneg_row[:].unsqueeze(1).to_broadcast([P, QS, HEADS]), ALU.mult).then_inc(sem("a_dt_done"), 1)

                    def a(b, par, q):
                        j, c = b * QS + q, q % 2
                        dve.wait_ge(sem("misc_filled"), j + 1)
                        nc.vector.tensor_tensor(cb[c][:], p_misc[:, CB], causal[:], ALU.mult).then_inc(sem("cb_done"), 1)
                        dve.wait_ge(sem("cb_done"), j + 1)
                        dve.wait_ge(sem("decay_done"), j + 1)
                        dve.wait_ge(sem("y_filled"), before(b, q))
                        nc.vector.tensor_tensor(mix[c][:], decay[c][:], cb[c][:].unsqueeze(1).to_broadcast([P, HEADS, P]), ALU.mult).then_inc(sem("mix_done"), 1)

                    def bb(b, par, q):
                        j, c = b * QS + q, q % 2
                        dve.wait_ge(sem("y_filled"), j + 1)
                        if q < QS - 1:
                            dve.wait_ge(sem("state_filled"), b * 3 + q + 1)
                            if q:
                                dve.wait_ge(sem("state_dec_done"), b * 2 + q)
                                nc.vector.tensor_tensor(state[:], state_dec[:], p_state[0:STATE, :].rearrange("p (h l) -> p h l", h=HEADS), ALU.add).then_inc(sem("state_done"), 1)
                            else:
                                nc.vector.tensor_copy(state[:], p_state[0:STATE, :].rearrange("p (h l) -> p h l", h=HEADS)).then_inc(sem("state_done"), 1)
                        dve.wait_ge(sem("yg_done"), j)
                        for h in range(HEADS):
                            last = nc.vector.scalar_tensor_tensor(y_sum[:, h, :], xbc[par][:, h, q * P:(q + 1) * P], d_row[:, h:h + 1], p_y[:, h * P:(h + 1) * P], ALU.mult, ALU.add)
                        last.then_inc(sem("y_sum_done"), 1)
                        dve.wait_ge(sem("y_sum_done"), j + 1)
                        dve.wait_ge(sem("yg_lo_done"), j)
                        dve.wait_ge(sem("ysq_done"), j)
                        nc.vector.tensor_tensor(yg[:], y_sum[:], gate_z[par][:, :, q * P:(q + 1) * P], ALU.mult).then_inc(sem("yg_done"), 1)

                    def v(b, par, q):
                        j = b * QS + q
                        dve.wait_ge(sem("v_filled"), j + 1)
                        nc.vector.bn_stats(st1[:], pa[0][:, 0:D_MODEL]).then_inc(sem("st1_done"), 1)
                        nc.vector.tensor_scalar(sse[:], pa[0][:, D_MODEL:D_MODEL + 1], 1.0 / D_INNER, LN_EPS, ALU.mult, ALU.add).then_inc(sem("sse_done"), 1)
                        dve.wait_ge(sem("st1_done"), j + 1)
                        hold(dve)
                        nc.vector.bn_aggr(mv1[:], st1[:]).then_inc(sem("mv1_done"), 1)
                        dve.wait_ge(sem("mv1_done"), j + 1)
                        dve.wait_ge(sem("sse_done"), j + 1)
                        nc.vector.scalar_tensor_tensor(ve1[:], sse[:], LN_EPS, mv1[:, 1:2], ALU.mult, ALU.add).then_inc(sem("ve1_done"), 1)

                    def r(b, par, q):
                        j, c = b * QS + q, q % 2
                        dve.wait_ge(sem("rs1_done"), j + 1)
                        nc.vector.tensor_scalar(shifted[:], pa[0][:, 0:D_MODEL], mv1[:, 0:1], rs1[:], ALU.subtract, ALU.mult).then_inc(sem("pa0_free"), 1)
                        dve.wait_ge(sem("pa0_free"), use_v(b, q))
                        dve.wait_ge(sem(f"res_loaded{c}"), (b * 2 + q // 2) * 16 + 16)
                        dve.wait_ge(sem(f"x1_stored{c}"), (b * 2 + q // 2) * 16)
                        nc.vector.tensor_tensor(x1[c][:], x_res[c][:], shifted[:], ALU.add).then_inc(sem(f"x1_done{c}"), 1)
                        dve.wait_ge(sem(f"x1_done{c}"), b * 2 + q // 2 + 1)
                        nc.vector.bn_stats(st2[:], x1[c][:]).then_inc(sem("st2_done"), 1)
                        dve.wait_ge(sem("st2_done"), j + 1)
                        hold(dve)
                        nc.vector.bn_aggr(mv2[:], st2[:]).then_inc(sem("mv2_done"), 1)
                        dve.wait_ge(sem("mv2_done"), j + 1)
                        nc.vector.tensor_scalar(ve2[:], mv2[:, 1:2], LN_EPS, None, ALU.add).then_inc(sem("ve2_done"), 1)

                    def n(b, par, q):
                        j, c = b * QS + q, q % 2
                        dve.wait_ge(sem("rs2_done"), j + 1)
                        dve.wait_ge(sem("t2_filled"), j)
                        nc.vector.tensor_scalar(xn2[:], x1[c][:], mv2[:, 0:1], rs2[:], ALU.subtract, ALU.mult).then_inc(sem("xn2_done"), 1)

                    def t(b, par, q):
                        j = b * QS + q
                        dve.wait_ge(sem("t2_hi_done"), j + 1)
                        part = bass.ds(j * P, P)
                        nc.vector.tensor_tensor(xt_lo[:, :, part], pa[1][:, 0:KD * P].rearrange("p (k n) -> p k n", k=KD), f32(xt_hi[:, :, part]), ALU.subtract).then_inc(sem("pa1_free"), 1)

                    walk({**nothing, "la": la, "lb": lb, "lc": lc, "s": s, "p": p, "a": a, "b": bb, "v": v, "r": r, "n": n, "t": t}, dve.Fori)

                @block.tensor
                def _(pe):
                    pe.wait_ge(sem("consts_loaded"), 16 * 5)
                    pe.wait_ge(sem("pool_consts"), 1)

                    def three(out, lh, ll, rh, rl, start, stop):
                        nc.tensor.matmul(out, lh, rh, start=start, stop=False)
                        nc.tensor.matmul(out, lh, rl, start=False, stop=False)
                        return nc.tensor.matmul(out, ll, rh, start=False, stop=stop)

                    def lc(b):
                        pe.wait_ge(sem("x_normed"), b + 1)
                        for k in range(KD):
                            pe.wait_ge(sem(f"pa{k}_free"), use_l(b, k) - 1)
                            for q in range(QS):
                                last = nc.tensor.transpose(pa[k][:, q * P:(q + 1) * P], x_norm[:, q, k * P:(k + 1) * P], ident[:])
                            last.then_inc(sem("xt_filled"), 1)

                    def s(b, par):
                        if isinstance(b, int) and b == 0:
                            pe.wait_ge(sem("win_lo_done"), 1)
                        for n, (kind, m) in enumerate(TILE_ORDER):
                            pe.wait_ge(sem(f"pa{n % 2}_free"), use_s(b, n) - 1)
                            if kind == "dt":
                                c0, w = DT_COL, HEADS
                            elif kind == "z":
                                c0, w = m * P, P
                            else:
                                c0, w = D_INNER + m * P, P
                            for k in range(KD):
                                part = bass.ds(b * SEQ, SEQ)
                                last = three(pa[n % 2][0:w, :], win_hi[:, k, c0:c0 + w], win_lo[:, k, c0:c0 + w],
                                             xt_hi[:, k, part], xt_lo[:, k, part], k == 0, k == KD - 1)
                            last.then_inc(sem("proj_filled"), 1)
                        if not (isinstance(b, int) and b == 0):
                            pe.wait_ge(sem("cb_done"), (b - 1) * QS)
                            pe.wait_ge(sem("b_tok_done"), (b - 1) * QS)
                        hold(pe)
                        for q in range(QS):
                            last = nc.tensor.transpose(p_misc[:, 192 + q * HEADS:192 + (q + 1) * HEADS], dt_rows[:, q * P:(q + 1) * P], ident[0:HEADS, 0:HEADS])
                        last.then_inc(sem("dtt_filled"), 1)

                    def a(b, par, q):
                        j, c = b * QS + q, q % 2
                        ts = slice(q * P, (q + 1) * P)
                        if q == 0:
                            if not (isinstance(b, int) and b == BATCH - 1):
                                pe.wait_ge(sem("dt_y_done"), b + 2)
                            pe.wait_ge(sem("silu_done"), (b + 1) * XBC_TILES)
                            pe.wait_ge(sem("a_dt_done"), b + 1)
                        pe.wait_ge(sem("cb_done"), j)
                        pe.wait_ge(sem("b_tok_done"), j)
                        if q == 0:
                            nc.tensor.matmul(p_misc[0:STATE, TOT], ones[:, 0:STATE], a_dt[par][:], start=True, stop=True).then_inc(sem("tot_filled"), 1)
                            pe.wait_ge(sem("carry_done"), b + 1)
                        nc.tensor.matmul(p_misc[:, CB], xbc[par][0:STATE, HEADS, ts], c_act[par][:, ts], start=True, stop=True)
                        nc.tensor.transpose(p_misc[:, BT], xbc[par][0:STATE, HEADS, ts], ident[0:STATE, 0:STATE]).then_inc(sem("misc_filled"), 1)
                        pe.wait_ge(sem("xs_done"), j)
                        for h in range(HEADS):
                            last = nc.tensor.transpose(p_xt[:, h * P:(h + 1) * P], xbc[par][:, h, ts], ident[:])
                        last.then_inc(sem("xt_tok_filled"), 1)
                        pe.wait_ge(sem("am_done"), j + 1)
                        pe.wait_ge(sem("decay_done"), j)
                        pe.wait_ge(sem("ce_done"), j)
                        for h in range(HEADS):
                            nc.tensor.matmul(p_seg[:, h * P:(h + 1) * P], am[c][:, h, 0:P], causal[:], start=True, stop=True)
                        for h in range(HEADS):
                            last = nc.tensor.matmul(p_cum[0:STATE, h * P:(h + 1) * P], am[c][:, h, P:], causal[:], start=True, stop=True)
                        last.then_inc(sem("seg_filled"), 1)

                    def bb(b, par, q):
                        j, c = b * QS + q, q % 2
                        pe.wait_ge(sem("xs_done"), j + 1)
                        pe.wait_ge(sem("mix_done"), j + 1)
                        pe.wait_ge(sem("y_sum_done"), j)
                        if q:
                            pe.wait_ge(sem("ce_c_done"), b * 3 + q)
                            pe.wait_ge(sem("state_done"), b * 3 + q)
                        for h in range(HEADS):
                            last = nc.tensor.matmul(p_y[:, h * P:(h + 1) * P], xs[c][:, h, :], mix[c][:, h, :], start=True, stop=(q == 0))
                            if q:
                                last = nc.tensor.matmul(p_y[:, h * P:(h + 1) * P], state[:, h, :], ce_c[c][:, h, :], start=False, stop=True)
                        last.then_inc(sem("y_filled"), 1)
                        if q < QS - 1:
                            pe.wait_ge(sem("xw_done"), b * 3 + q + 1)
                            pe.wait_ge(sem("b_tok_done"), j + 1)
                            pe.wait_ge(sem("state_done"), b * 3 + q)
                            nc.tensor.matmul(p_state[0:STATE, :], b_tok[c][:], xw[:].rearrange("p h l -> p (h l)"), start=True, stop=True).then_inc(sem("state_filled"), 1)

                    def v(b, par, q):
                        j, c = b * QS + q, q % 2
                        if isinstance(b, int) and b == 0 and q == 0:
                            pe.wait_ge(sem("wo_lo_done"), 1)
                        pe.wait_ge(sem("pa0_free"), use_v(b, q) - 1)
                        pe.wait_ge(sem("ysq_done"), j + 1)
                        pe.wait_ge(sem("yg_lo_done"), j + 1)
                        for h in range(HEADS):
                            nc.tensor.matmul(pa[0][:, D_MODEL:D_MODEL + 1], ysq[:, h, :], ones[:, 0:1], start=(h == 0), stop=(h == HEADS - 1))
                        for h in range(HEADS):
                            last = three(pa[0][:, 0:D_MODEL], yg_hi[c][:, h, :], yg_lo[c][:, h, :], wo_hi[:, h, :], wo_lo[:, h, :], h == 0, h == HEADS - 1)
                        last.then_inc(sem("v_filled"), 1)

                    def t(b, par, q):
                        j = b * QS + q
                        pe.wait_ge(sem("xn2_done"), j + 1)
                        pe.wait_ge(sem("pa1_free"), use_t(b, q) - 1)
                        for k in range(KD):
                            last = nc.tensor.transpose(pa[1][:, k * P:(k + 1) * P], xn2[:, k * P:(k + 1) * P], ident[:])
                        last.then_inc(sem("t2_filled"), 1)

                    walk({**nothing, "lc": lc, "s": s, "a": a, "b": bb, "v": v, "t": t}, pe.Fori)

        with ExitStack() as st:
            comb_t = alloc(st, "comb_t", [PARTS * GATES, TOKENS], BF16)
            spread = alloc(st, "spread", [PARTS * GATES, CHUNKS, P], BF16)
            ident_b = alloc(st, "ident_b", [P, P], BF16)
            acc = alloc(st, "acc", [P, TILES, D_MODEL])

            with ExitStack() as rt:
                logit_rows = [alloc(rt, f"logit_rows{i}", [GATES, SEQ]) for i in range(2)]
                logits = alloc(rt, "logits", [P, TILES, GATES])
                index = alloc(rt, "index", [P, EXPERTS])
                top = alloc(rt, "top", [P, TILES])
                shifted2 = alloc(rt, "shifted2", [P, TILES, EXPERTS])
                expd = alloc(rt, "expd", [P, TILES, EXPERTS])
                total = alloc(rt, "total", [P, TILES])
                rtotal = alloc(rt, "rtotal", [P, TILES])
                probs = alloc(rt, "probs", [P, TILES, EXPERTS])
                top8 = alloc(rt, "top8", [P, TILES, 8])
                idx8 = alloc(rt, "idx8", [P, TILES, 8], U32)
                idxf = alloc(rt, "idxf", [P, TILES, 8])
                hit = [alloc(rt, f"hit{i}", [P, TILES, EXPERTS]) for i in range(TOP_K)]
                kept = alloc(rt, "kept", [P, TILES])
                kept_c = alloc(rt, "kept_c", [P, TILES])
                rkept = alloc(rt, "rkept", [P, TILES])
                chosen = alloc(rt, "chosen", [P, TILES, EXPERTS])
                sg_e = alloc(rt, "sg_e", [P, TILES])
                sg_1 = alloc(rt, "sg_1", [P, TILES])
                comb = alloc(rt, "comb", [P, TILES, GATES])
                rest = [alloc(rt, f"rest{i}", [P, TILES, GATES]) for i in range(2)]
                parts = alloc(rt, "parts", [P, TILES, PARTS * GATES], BF16)
                p_logit = [rt.enter_context(nc.psum_tensor(f"p_logit{i}", [P, 512], F32)) for i in range(2)]
                p_tok = [rt.enter_context(nc.psum_tensor(f"p_tok{i}", [P, 512], F32)) for i in range(2)]
                p_comb = [rt.enter_context(nc.psum_tensor(f"p_comb{i}", [P, 1024], BF16)) for i in range(2)]
                CT = 8

                with nc.Block() as block:
                    @block.sync
                    def _(sp):
                        for dst, src in ((index[:], index_d), (spread[:], spread_d.bitcast(BF16))):
                            sp.dma_start(dst, src).then_inc(sem("router_consts"), 16)

                    @block.scalar
                    def _(act):
                        with act.Fori(0, BATCH // 2) as p:
                            for i in range(2):
                                act.wait_ge(sem(f"logit_filled{i}"), p + 1)
                                act.wait_ge(sem(f"logit_turned{i}"), p)
                                nc.scalar.activation(logit_rows[i][:], p_logit[i][0:GATES, :], ACT.Copy).then_inc(sem(f"logit_rows_done{i}"), 1)
                        act.wait_ge(sem("shifted2_done"), 1)
                        nc.scalar.activation(expd[:], shifted2[:], ACT.Exp)
                        nc.scalar.activation(sg_e[:].unsqueeze(2), logits[:, :, EXPERTS:], ACT.Exp, scale=-1.0).then_inc(sem("exps_done"), 1)
                        for r in range(TILES // CT):
                            act.wait_ge(sem("comb_turned"), r + 1)
                            nc.scalar.activation(comb_t[:, r * CT * P:(r + 1) * CT * P], p_comb[r % 2][0:PARTS * GATES, :], ACT.Copy).then_inc(sem("comb_t_done"), 1)

                    @block.vector
                    def _(dve):
                        steps = [0]

                        def then(ins):
                            steps[0] += 1
                            ins.then_inc(sem("router_step"), 1)
                            dve.wait_ge(sem("router_step"), steps[0])

                        def wide(ap, n):
                            return ap.unsqueeze(2).to_broadcast([P, TILES, n])

                        nc.vector.tensor_copy(ident_b[:], ident[:]).then_inc(sem("ident_b_done"), 1)
                        with dve.Fori(0, BATCH // 2) as p:
                            for i in range(2):
                                dve.wait_ge(sem(f"logit_turned{i}"), p + 1)
                                nc.vector.tensor_copy(logits[:, bass.ds((p * 2 + i) * QS, QS), :], p_tok[i][:, 0:QS * GATES].rearrange("p (q e) -> p q e", q=QS)).then_inc(sem(f"logits_done{i}"), 1)
                        for i in range(2):
                            dve.wait_ge(sem(f"logits_done{i}"), BATCH // 2)
                        then(nc.vector.tensor_reduce(top[:], logits[:, :, 0:EXPERTS], AX.X, ALU.max))
                        nc.vector.tensor_tensor(shifted2[:], logits[:, :, 0:EXPERTS], wide(top[:], EXPERTS), ALU.subtract).then_inc(sem("shifted2_done"), 1)
                        dve.wait_ge(sem("exps_done"), 1)
                        then(nc.vector.tensor_reduce(total[:], expd[:], AX.X, ALU.add))
                        then(nc.vector.reciprocal(rtotal[:], total[:]))
                        then(nc.vector.tensor_tensor(probs[:], expd[:], wide(rtotal[:], EXPERTS), ALU.mult))
                        for t in range(TILES):
                            last = nc.vector.max(top8[:, t, :], probs[:, t, :])
                        then(last)
                        for t in range(TILES):
                            last = nc.vector.max_index(idx8[:, t, :], top8[:, t, :], probs[:, t, :])
                        then(last)
                        then(nc.vector.tensor_copy(idxf[:], idx8[:]))
                        dve.wait_ge(sem("router_consts"), 32)
                        for k in range(TOP_K):
                            last = nc.vector.tensor_tensor(hit[k][:], index[:].unsqueeze(1).to_broadcast([P, TILES, EXPERTS]), wide(idxf[:, :, k], EXPERTS), ALU.is_equal)
                        then(last)
                        nc.vector.tensor_tensor(hit[0][:], hit[0][:], hit[1][:], ALU.add)
                        then(nc.vector.tensor_tensor(hit[2][:], hit[2][:], hit[3][:], ALU.add))
                        then(nc.vector.tensor_tensor(hit[1][:], hit[0][:], hit[2][:], ALU.add))
                        then(nc.vector.tensor_tensor(chosen[:], probs[:], hit[1][:], ALU.mult))
                        then(nc.vector.tensor_reduce(kept[:], top8[:, :, 0:TOP_K], AX.X, ALU.add))
                        then(nc.vector.tensor_scalar(kept_c[:], kept[:], 1e-9, None, ALU.max))
                        then(nc.vector.reciprocal(rkept[:], kept_c[:]))
                        nc.vector.tensor_tensor(comb[:, :, 0:EXPERTS], chosen[:], wide(rkept[:], EXPERTS), ALU.mult)
                        then(nc.vector.tensor_scalar(sg_1[:], sg_e[:], 1.0, None, ALU.add))
                        then(nc.vector.reciprocal(comb[:, :, EXPERTS:], sg_1[:].unsqueeze(2)))
                        then(nc.vector.tensor_copy(parts[:, :, 0:GATES], comb[:]))
                        then(nc.vector.tensor_tensor(rest[0][:], comb[:], parts[:, :, 0:GATES], ALU.subtract))
                        then(nc.vector.tensor_copy(parts[:, :, GATES:2 * GATES], rest[0][:]))
                        then(nc.vector.tensor_tensor(rest[1][:], rest[0][:], parts[:, :, GATES:2 * GATES], ALU.subtract))
                        nc.vector.tensor_copy(parts[:, :, 2 * GATES:], rest[1][:]).then_inc(sem("parts_done"), 1)

                    @block.gpsimd
                    def _(pool):
                        nc.gpsimd.memset(acc[:], 0.0).then_inc(sem("acc_zero"), 1)

                    @block.tensor
                    def _(pe):
                        def logit_cols(p, i):
                            part = bass.ds((p * 2 + i) * SEQ, SEQ)
                            for k in range(KD):
                                nc.tensor.matmul(p_logit[i][0:GATES, :], rw_hi[:, k, :], xt_hi[:, k, part], start=(k == 0), stop=False)
                                nc.tensor.matmul(p_logit[i][0:GATES, :], rw_hi[:, k, :], xt_lo[:, k, part], start=False, stop=False)
                                last = nc.tensor.matmul(p_logit[i][0:GATES, :], rw_lo[:, k, :], xt_hi[:, k, part], start=False, stop=(k == KD - 1))
                            last.then_inc(sem(f"logit_filled{i}"), 1)

                        with pe.Fori(0, BATCH // 2) as p:
                            for i in range(2):
                                pe.wait_ge(sem(f"logit_rows_done{i}"), p)
                                logit_cols(p, i)
                            for i in range(2):
                                pe.wait_ge(sem(f"logit_rows_done{i}"), p + 1)
                                pe.wait_ge(sem(f"logits_done{i}"), p)
                                hold(pe)
                                for q in range(QS):
                                    last = nc.tensor.transpose(p_tok[i][:, q * GATES:(q + 1) * GATES], logit_rows[i][:, q * P:(q + 1) * P], ident[0:GATES, 0:GATES])
                                last.then_inc(sem(f"logit_turned{i}"), 1)
                        pe.wait_ge(sem("ident_b_done"), 1)
                        pe.wait_ge(sem("parts_done"), 1)
                        for r in range(TILES // CT):
                            if r >= 2:
                                pe.wait_ge(sem("comb_t_done"), r - 1)
                            for t in range(CT):
                                last = nc.tensor.transpose(p_comb[r % 2][0:PARTS * GATES, t * P:(t + 1) * P], parts[:, r * CT + t, :], ident_b[:])
                            last.then_inc(sem("comb_turned"), 1)

            with ExitStack() as mo:
                raw = [alloc(mo, f"raw{c}", [P, W_COLS]) for c in range(GROUP)]
                w_hi = [[alloc(mo, f"w_hi{h}{c}", [P, W_COLS], F32R) for c in range(GROUP)] for h in range(2)]
                w_lo = [[alloc(mo, f"w_lo{h}{c}", [P, W_COLS], F32R) for c in range(GROUP)] for h in range(2)]
                silu_g = [alloc(mo, f"silu_g{c}", [P, SEQ]) for c in range(GROUP)]
                weighted = [alloc(mo, f"weighted{c}", [P, SEQ]) for c in range(GROUP)]
                hidden = [alloc(mo, f"hidden{c}", [P, SEQ]) for c in range(GROUP)]
                h_hi = [alloc(mo, f"h_hi{c}", [P, SEQ], F32R) for c in range(GROUP)]
                h_lo = [alloc(mo, f"h_lo{c}", [P, SEQ], F32R) for c in range(GROUP)]
                partial = alloc(mo, "partial", [P, QS, D_MODEL])

                def mbank(name, n=512):
                    return mo.enter_context(nc.psum_tensor(name, [P, n], F32))

                p_g = [mbank(f"p_g{c}") for c in range(GROUP)]
                p_c = [mbank(f"p_c{c}") for c in range(GROUP)]
                p_u = [mbank(f"p_u{c}") for c in range(GROUP)]
                p_out = [mbank(f"p_out{i}") for i in range(2)]

                def walk_experts(stages, loop):
                    prep, up, down = stages["prep"], stages["up"], stages["down"]

                    def step(g, half, t, ahead):
                        up(g, half, t, 1)
                        down(g, half, t, 0)
                        if ahead:
                            up(*ahead, 0)
                        down(g, half, t, 1)

                    def pair(pp, final):
                        for half in range(2):
                            g = pp * 2 + half
                            more = not (final and half)
                            if more:
                                prep(g + 1, 1 - half, pp + half)
                            with loop(0, BATCH - 1) as t:
                                step(g, half, t, (g, half, t + 1))
                            step(g, half, BATCH - 1, (g + 1, 1 - half, 0) if more else None)

                    prep(0, 0, 0)
                    up(0, 0, 0, 0)
                    with loop(0, GROUPS // 2 - 1) as pp:
                        pair(pp, False)
                    pair(GROUPS // 2 - 1, True)

                idle = {"prep": lambda *a: None, "up": lambda *a: None, "down": lambda *a: None}

                with nc.Block() as block:
                    @block.sync
                    def _(sp):
                        with sp.Fori(0, GROUPS) as g:
                            for c in range(GROUP):
                                sp.wait_ge(sem(f"w_ready{c}"), g)
                                sp.dma_start(raw[c][:], moe_w[bass.ds(g * GROUP + c, 1)].rearrange("a p n -> (a p) n")).then_inc(sem(f"raw_loaded{c}"), 16)

                    @block.scalar
                    def _(act):
                        def prep(g, half, uses):
                            act.wait_ge(sem(f"group_done{half}"), uses)
                            for c in range(GROUP):
                                act.wait_ge(sem(f"raw_loaded{c}"), g * 16 + 16)
                                nc.scalar.activation(w_hi[half][c][:], raw[c][:], ACT.Copy).then_inc(sem(f"w_hi_done{c}"), 1)

                        def up(g, half, t, c):
                            i = g * BATCH + t
                            act.wait_ge(sem(f"g_filled{c}"), i + 1)
                            act.wait_ge(sem(f"weighted_done{c}"), i)
                            nc.scalar.activation(silu_g[c][:], p_g[c][:], ACT.Silu).then_inc(sem(f"silu_g_done{c}"), 1)

                        def down(g, half, t, c):
                            if c == 0:
                                return
                            i = g * BATCH + t
                            act.wait_ge(sem("down_done1"), i + 1)
                            act.wait_ge(sem("acc_done"), i)
                            for o in range(2):
                                last = nc.scalar.activation(partial[:, 2 * o:2 * o + 2, :], p_out[o][:].rearrange("p (q n) -> p q n", q=2), ACT.Copy)
                            last.then_inc(sem("partial_done"), 1)

                        walk_experts({"prep": prep, "up": up, "down": down}, act.Fori)

                    @block.gpsimd
                    def _(pool):
                        def prep(g, half, uses):
                            for c in range(GROUP):
                                pool.wait_ge(sem(f"w_hi_done{c}"), g + 1)
                                nc.gpsimd.tensor_tensor(w_lo[half][c][:], raw[c][:], f32(w_hi[half][c][:]), ALU.subtract).then_inc(sem(f"w_ready{c}"), 1)

                        def down(g, half, t, c):
                            if c == 0:
                                return
                            i = g * BATCH + t
                            pool.wait_ge(sem("partial_done"), i + 1)
                            part = acc[:, bass.ds(t * QS, QS), :]
                            nc.gpsimd.tensor_tensor(part, part, partial[:], ALU.add).then_inc(sem("acc_done"), 1)

                        walk_experts({**idle, "prep": prep, "down": down}, pool.Fori)

                    @block.vector
                    def _(dve):
                        def up(g, half, t, c):
                            i = g * BATCH + t
                            dve.wait_ge(sem(f"silu_g_done{c}"), i + 1)
                            dve.wait_ge(sem(f"c_filled{c}"), i + 1)
                            nc.vector.tensor_tensor(weighted[c][:], silu_g[c][:], p_c[c][:], ALU.mult).then_inc(sem(f"weighted_done{c}"), 1)
                            dve.wait_ge(sem(f"weighted_done{c}"), i + 1)
                            dve.wait_ge(sem(f"u_filled{c}"), i + 1)
                            nc.vector.tensor_tensor(hidden[c][:], weighted[c][:], p_u[c][:], ALU.mult).then_inc(sem(f"hidden_done{c}"), 1)
                            dve.wait_ge(sem(f"hidden_done{c}"), i + 1)
                            dve.wait_ge(sem(f"down_done{c}"), i)
                            nc.vector.tensor_copy(h_hi[c][:], hidden[c][:]).then_inc(sem(f"h_hi_done{c}"), 1)
                            dve.wait_ge(sem(f"h_hi_done{c}"), i + 1)
                            nc.vector.tensor_tensor(h_lo[c][:], hidden[c][:], f32(h_hi[c][:]), ALU.subtract).then_inc(sem(f"h_lo_done{c}"), 1)

                        walk_experts({**idle, "up": up}, dve.Fori)

                    @block.tensor
                    def _(pe):
                        def up(g, half, t, c):
                            i = g * BATCH + t
                            part = bass.ds(t * SEQ, SEQ)
                            chunk_g = g * GROUP + c
                            pe.wait_ge(sem(f"w_ready{c}"), g + 1)

                            def project(bank, off):
                                for k in range(KD):
                                    cols = slice(off + k * P, off + (k + 1) * P)
                                    hi, lo = w_hi[half][c][:, cols], w_lo[half][c][:, cols]
                                    nc.tensor.matmul(bank[:], hi, xt_hi[:, k, part], start=(k == 0), stop=False)
                                    nc.tensor.matmul(bank[:], hi, xt_lo[:, k, part], start=False, stop=False)
                                    last = nc.tensor.matmul(bank[:], lo, xt_hi[:, k, part], start=False, stop=(k == KD - 1))
                                return last

                            pe.wait_ge(sem(f"silu_g_done{c}"), i)
                            project(p_g[c], G_OFF).then_inc(sem(f"g_filled{c}"), 1)
                            pe.wait_ge(sem(f"weighted_done{c}"), i)
                            nc.tensor.matmul(p_c[c][:], spread[:, bass.ds(chunk_g, 1), :].rearrange("r a p -> r (a p)"), comb_t[:, part], start=True, stop=True).then_inc(sem(f"c_filled{c}"), 1)
                            pe.wait_ge(sem(f"hidden_done{c}"), i)
                            project(p_u[c], U_OFF).then_inc(sem(f"u_filled{c}"), 1)

                        def down(g, half, t, c):
                            i = g * BATCH + t
                            pe.wait_ge(sem(f"h_hi_done{c}"), i + 1)
                            if c == 0:
                                pe.wait_ge(sem("partial_done"), i)
                            wd_hi, wd_lo = w_hi[half][c][:, D_OFF:], w_lo[half][c][:, D_OFF:]

                            def out(q):
                                return p_out[q // 2][:, (q % 2) * D_MODEL:(q % 2 + 1) * D_MODEL]

                            for q in range(QS):
                                cols = slice(q * P, (q + 1) * P)
                                nc.tensor.matmul(out(q), h_hi[c][:, cols], wd_hi, start=(c == 0 and q % 2 == 0), stop=False, skip_group_check=True)
                                nc.tensor.matmul(out(q), h_hi[c][:, cols], wd_lo, start=False, stop=False, skip_group_check=True)
                            pe.wait_ge(sem(f"h_lo_done{c}"), i + 1)
                            for q in range(QS):
                                last = nc.tensor.matmul(out(q), h_lo[c][:, q * P:(q + 1) * P], wd_hi, start=False, stop=(c == GROUP - 1), skip_group_check=True)
                            last.then_inc(sem(f"down_done{c}"), 1)
                            if c == GROUP - 1 and isinstance(t, int):
                                pe.wait_ge(sem(f"down_done{c}"), i + 1)
                                pe.sem_inc(sem(f"group_done{half}"), 1)

                        walk_experts({**idle, "up": up, "down": down}, pe.Fori)

            with ExitStack() as fi:
                x1_in = [alloc(fi, f"x1_in{i}", [P, QS, D_MODEL]) for i in range(2)]
                normed = [alloc(fi, f"normed{i}", [P, QS, D_MODEL]) for i in range(2)]
                final = [alloc(fi, f"final{i}", [P, QS, D_MODEL]) for i in range(2)]
                stf = [alloc(fi, f"stf{i}", [P, QS, 6]) for i in range(2)]
                mvf = [alloc(fi, f"mvf{i}", [P, QS, 2]) for i in range(2)]
                vef = [alloc(fi, f"vef{i}", [P, QS]) for i in range(2)]
                rsf = [alloc(fi, f"rsf{i}", [P, QS]) for i in range(2)]
                x1_v = x1_dram.rearrange("(b q) p d -> b p q d", q=QS)
                out_v = out.rearrange("b (q p) d -> b p q d", p=P)
                with nc.Block() as block:
                    @block.sync
                    def _(sp):
                        with sp.Fori(0, BATCH // 2) as p:
                            for i in range(2):
                                sp.wait_ge(sem(f"final_done{i}"), p)
                                sp.dma_start(x1_in[i][:], x1_v[bass.ds(p * 2 + i, 1)].rearrange("a p q d -> (a p) q d")).then_inc(sem(f"x1_back{i}"), 16)

                    @block.scalar
                    def _(act):
                        with act.Fori(0, BATCH // 2) as p:
                            for i in range(2):
                                act.wait_ge(sem(f"final_done{i}"), p + 1)
                                act.dma_start(out_v[bass.ds(p * 2 + i, 1)].rearrange("a p q d -> (a p) q d"), final[i][:]).then_inc(sem(f"out_stored{i}"), 16)
                        for i in range(2):
                            act.wait_ge(sem(f"out_stored{i}"), 16 * (BATCH // 2))

                    @block.gpsimd
                    def _(pool):
                        with pool.Fori(0, BATCH // 2) as p:
                            for i in range(2):
                                pool.wait_ge(sem(f"vef_done{i}"), p + 1)
                                nc.gpsimd.tensor_tensor(rsf[i][:], vef[i][:], exponent[:], ALU.pow).then_inc(sem(f"rsf_done{i}"), 1)

                    @block.vector
                    def _(dve):
                        with dve.Fori(0, BATCH // 2) as p:
                            for i in range(2):
                                for q in range(QS):
                                    last = nc.vector.bn_stats(stf[i][:, q, :], acc[:, bass.ds((p * 2 + i) * QS + q, 1), :].rearrange("p a d -> p (a d)"))
                                last.then_inc(sem(f"stf_done{i}"), 1)
                                dve.wait_ge(sem(f"stf_done{i}"), p + 1)
                                hold(dve)
                                for q in range(QS):
                                    last = nc.vector.bn_aggr(mvf[i][:, q, :], stf[i][:, q, :])
                                last.then_inc(sem(f"mvf_done{i}"), 1)
                                dve.wait_ge(sem(f"mvf_done{i}"), p + 1)
                                nc.vector.tensor_scalar(vef[i][:].unsqueeze(2), mvf[i][:, :, 1:2], LN_EPS, None, ALU.add).then_inc(sem(f"vef_done{i}"), 1)
                            for i in range(2):
                                dve.wait_ge(sem(f"rsf_done{i}"), p + 1)
                                for q in range(QS):
                                    last = nc.vector.tensor_scalar(normed[i][:, q, :], acc[:, bass.ds((p * 2 + i) * QS + q, 1), :].rearrange("p a d -> p (a d)"), mvf[i][:, q, 0:1], rsf[i][:, q:q + 1], ALU.subtract, ALU.mult)
                                last.then_inc(sem(f"normed_done{i}"), 1)
                                dve.wait_ge(sem(f"normed_done{i}"), p + 1)
                                dve.wait_ge(sem(f"x1_back{i}"), p * 16 + 16)
                                dve.wait_ge(sem(f"out_stored{i}"), p * 16)
                                nc.vector.tensor_tensor(final[i][:], normed[i][:], x1_in[i][:], ALU.add).then_inc(sem(f"final_done{i}"), 1)


_SHAPE_CONSTS = ("ident", "causal", "later", "index", "spread")


def _layout(inputs):
    def of(name):
        return np.asarray(inputs["L0_" + name])

    wide = ROUTED_CHUNKS * P
    routed = [np.transpose(of("ffn_w_" + n), (1, 0, 2)).reshape(D_MODEL, wide) for n in ("gate", "up")]
    pad = SHARED_CHUNKS * P - I_SHARED
    shared = [np.pad(of("ffn_sh_" + n), ((0, 0), (0, pad))) for n in ("gate", "up")]
    ups = [np.concatenate([r, s], axis=1).reshape(KD, P, CHUNKS, P) for r, s in zip(routed, shared)]
    down = np.concatenate([of("ffn_w_down").reshape(wide, D_MODEL),
                           np.pad(of("ffn_sh_down"), ((0, pad), (0, 0)))]).reshape(CHUNKS, P, D_MODEL)
    moe = np.concatenate([np.transpose(w, (2, 1, 0, 3)).reshape(CHUNKS, P, KD * P) for w in ups] + [down], axis=2)
    gates = np.concatenate([of("ffn_router_w").T, of("ffn_sh_gate_w")], axis=1)
    t = np.arange(P)
    causal = (t[:, None] <= t[None, :]).astype(np.float32)
    later = np.concatenate([1 - causal.T, np.ones((P, STATE), np.float32)], axis=1)
    later[:, :P] = (t[:, None] > t[None, :]).astype(np.float32)
    unit = np.arange(CHUNKS * P)
    gate_of = np.minimum(unit // I_MOE, EXPERTS)
    one = (np.arange(GATES)[:, None] == gate_of[None, :]).astype(np.float32)
    spread = (np.tile(one, (PARTS, 1)).view(np.uint32) >> 16).astype(np.uint16).reshape(PARTS * GATES, CHUNKS, P)
    index = np.tile(np.arange(EXPERTS, dtype=np.float32), (P, 1))
    small = np.concatenate(
        [np.transpose(of("attn_conv_w").reshape(XBC_TILES, P, TAPS), (1, 0, 2)).reshape(P, -1),
         of("attn_conv_b").reshape(XBC_TILES, P).T, of("attn_norm_w").reshape(HEADS, P).T]
        + [np.tile(of("attn_" + n), (P, 1)) for n in ("dt_bias", "A_log", "D")], axis=1)
    return {**{"attn_" + n: of("attn_" + n) for n in ("u", "W_in", "W_out")}, "small": small, "gates": gates, "moe": moe,
            "ident": np.eye(P, dtype=np.float32), "causal": causal, "later": later, "index": index, "spread": spread}


def kernel(**inputs):
    import concourse.bacc as bacc
    from concourse.bass_utils import run_bass_kernel_spmd

    nc = bacc.Bacc("TRN2", target_bir_lowering=False, num_devices=1)
    arrays, args = {}, []
    for name, a in _layout(inputs).items():
        a = np.ascontiguousarray(a)
        arrays[f"in_{name}"] = a
        args.append(nc.dram_tensor(f"in_{name}", a.shape, mybir.dt.from_np(a.dtype), kind="ExternalInput").ap())
    args.append(nc.dram_tensor("out_0", (BATCH, SEQ, D_MODEL), mybir.dt.float32, kind="ExternalOutput").ap())
    sandwich_kernel(nc, *args)
    r = run_bass_kernel_spmd(nc, [arrays], core_ids=[0])
    return np.asarray(r.results[0]["out_0"])
```

```python
import numpy as np
import concourse.bass as bass
from concourse import mybir
from contextlib import ExitStack

BATCH, SEQ, D_MODEL = 8, 512, 256
TOKENS = BATCH * SEQ
HEADS, HEAD_DIM, STATE = 4, 128, 64
D_INNER = HEADS * HEAD_DIM
TAPS = 4
EXPERTS, TOP_K, I_MOE, I_SHARED = 16, 4, 176, 704
LN_EPS = 1e-5

P = 128
KD = D_MODEL // P
CHUNK = 128
QS = SEQ // CHUNK
TILES = TOKENS // P
GATES = EXPERTS + 1
PARTS = 3
XBC_TILES = (D_INNER + 2 * STATE) // P
W_IN_COLS = 2 * D_INNER + 2 * STATE + HEADS
DT_COL = W_IN_COLS - HEADS
ROUTED_CHUNKS = EXPERTS * I_MOE // P
SHARED_CHUNKS = -(-I_SHARED // P)
CHUNKS = ROUTED_CHUNKS + SHARED_CHUNKS
GROUP = 2
GROUPS = CHUNKS // GROUP
W_COLS = KD * P * 2 + D_MODEL
G_OFF, U_OFF, D_OFF = 0, KD * P, 2 * KD * P


def sandwich_kernel(nc, u, w_in, w_out, small_d,
                    gates_w, moe_w, ident_d, causal_d, later_d, index_d, spread_d, out):
    F32, F32R, BF16, U32 = mybir.dt.float32, mybir.dt.float32r, mybir.dt.bfloat16, mybir.dt.uint32
    ALU, ACT, AX = mybir.AluOpType, mybir.ActivationFunctionType, mybir.AxisListType

    whole = ExitStack()
    sems = {}

    def sem(name):
        if name not in sems:
            sems[name] = whole.enter_context(nc.semaphore(name))
        return sems[name]

    def hold(engine):
        engine.sem_inc(sem("held"), 1)

    def f32(ap):
        return ap.bitcast(F32)

    with whole:
        x1_dram = nc.dram_tensor("x1_scratch", (TILES, P, D_MODEL), F32, kind="Internal").ap()

        def alloc(stack, name, shape, dt=F32):
            return stack.enter_context(nc.sbuf_tensor(name, shape, dt))

        xt_hi = alloc(whole, "xt_hi", [P, KD, TOKENS], F32R)
        xt_lo = alloc(whole, "xt_lo", [P, KD, TOKENS], F32R)
        ident = alloc(whole, "ident", [P, P])
        exponent = alloc(whole, "exponent", [P, QS])
        rw_hi = alloc(whole, "rw_hi", [P, KD, GATES], F32R)
        rw_lo = alloc(whole, "rw_lo", [P, KD, GATES], F32R)

        with ExitStack() as st:
            win_hi = alloc(st, "win_hi", [P, KD, W_IN_COLS], F32R)
            win_lo = alloc(st, "win_lo", [P, KD, W_IN_COLS], F32R)
            wo_hi = alloc(st, "wo_hi", [P, HEADS, D_MODEL], F32R)
            wo_lo = alloc(st, "wo_lo", [P, HEADS, D_MODEL], F32R)
            rw_raw = alloc(st, "rw_raw", [P, KD, GATES])
            causal = alloc(st, "causal", [P, P])
            later = alloc(st, "later", [P, P])
            ones = alloc(st, "ones", [P, P])
            small = alloc(st, "small", [P, XBC_TILES * (TAPS + 1) + 4 * HEADS])
            conv_taps = small[:, 0:XBC_TILES * TAPS].rearrange("p (m k) -> p m k", k=TAPS)
            after = XBC_TILES * TAPS
            conv_bias = small[:, after:after + XBC_TILES]
            after += XBC_TILES
            norm_col, dtb_row, alog_row, d_row = (
                small[:, after + i * HEADS:after + (i + 1) * HEADS] for i in range(4))
            aneg_row = alloc(st, "aneg_row", [P, HEADS])
            xbc = [alloc(st, f"xbc{i}", [P, XBC_TILES, SEQ]) for i in range(2)]
            c_act = [alloc(st, f"c_act{i}", [P, SEQ]) for i in range(2)]
            gate_z = [alloc(st, f"gate_z{i}", [P, HEADS, SEQ]) for i in range(2)]
            conv_in = [alloc(st, f"conv_in{i}", [P, TAPS - 1 + SEQ]) for i in range(2)]
            conv_acc = [alloc(st, f"conv_acc{i}", [P, SEQ]) for i in range(2)]
            dt_rows = alloc(st, "dt_rows", [HEADS, SEQ])
            dt_y = alloc(st, "dt_y", [P, QS * HEADS])
            dt_neg = alloc(st, "dt_neg", [P, QS * HEADS])
            dt_nabs = alloc(st, "dt_nabs", [P, QS * HEADS])
            dt_e = alloc(st, "dt_e", [P, QS * HEADS])
            dt_l = alloc(st, "dt_l", [P, QS * HEADS])
            dt = [alloc(st, f"dt{i}", [P, QS * HEADS]) for i in range(2)]
            a_dt = [alloc(st, f"a_dt{i}", [P, QS * HEADS]) for i in range(2)]
            carry = [alloc(st, f"carry{i}", [P, QS * 2]) for i in range(2)]
            x_in = alloc(st, "x_in", [P, QS, D_MODEL])
            x_norm = alloc(st, "x_norm", [P, QS, D_MODEL])
            st0 = alloc(st, "st0", [P, QS, 6])
            mv0 = alloc(st, "mv0", [P, QS, 2])
            ve0 = alloc(st, "ve0", [P, QS])
            rs0 = alloc(st, "rs0", [P, QS])
            am = [alloc(st, f"am{i}", [P, HEADS, P]) for i in range(2)]
            am_all = [alloc(st, f"am_all{i}", [P, 2, 2, STATE]) for i in range(2)]
            decay = [alloc(st, f"decay{i}", [P, HEADS, P]) for i in range(2)]
            mix = [alloc(st, f"mix{i}", [P, HEADS, P]) for i in range(2)]
            xs = [alloc(st, f"xs{i}", [P, HEADS, P]) for i in range(2)]
            xw = alloc(st, "xw", [P, HEADS, P])
            cb = [alloc(st, f"cb{i}", [P, P]) for i in range(2)]
            ce = [alloc(st, f"ce{i}", [P, 2, P]) for i in range(2)]
            b_tok = [alloc(st, f"b_tok{i}", [P, STATE]) for i in range(2)]
            state = alloc(st, "state", [P, 2, P])
            state_dec = alloc(st, "state_dec", [P, 2, P])
            xd = [alloc(st, f"xd{i}", [P, HEADS, P]) for i in range(2)]
            y_sum = alloc(st, "y_sum", [P, HEADS, P])
            yg = alloc(st, "yg", [P, HEADS, P])
            yg_hi = [alloc(st, f"yg_hi{i}", [P, HEADS, P], F32R) for i in range(2)]
            yg_lo = [alloc(st, f"yg_lo{i}", [P, HEADS, P], F32R) for i in range(2)]
            ysq = alloc(st, "ysq", [P, HEADS, P])
            sq_pair = alloc(st, "sq_pair", [P, 2, P])
            sq_sum = [alloc(st, f"sq_sum{i}", [P, P]) for i in range(2)]
            x_res = [alloc(st, f"x_res{i}", [P, D_MODEL]) for i in range(2)]
            shifted = alloc(st, "shifted", [P, D_MODEL])
            x1 = [alloc(st, f"x1_{i}", [P, D_MODEL]) for i in range(2)]
            xn2 = alloc(st, "xn2", [P, D_MODEL])
            st1 = alloc(st, "st1", [P, 6]); mv1 = alloc(st, "mv1", [P, 2])
            sse = alloc(st, "sse", [P, 1]); ve1 = alloc(st, "ve1", [P, 1]); rs1 = alloc(st, "rs1", [P, 1])
            st2 = alloc(st, "st2", [P, 6]); mv2 = alloc(st, "mv2", [P, 2])
            ve2 = alloc(st, "ve2", [P, 1]); rs2 = alloc(st, "rs2", [P, 1])
            win_raw = xbc[1][:].rearrange("p a b -> p (a b)")[:, 0:KD * W_IN_COLS].rearrange(
                "p (k n) -> p k n", k=KD)
            wo_raw = gate_z[1][:].rearrange("p a b -> p (a b)")[:, 0:HEADS * D_MODEL].rearrange(
                "p (k n) -> p k n", k=HEADS)

            wo_scaled = gate_z[1][:].rearrange("p a b -> p (a b)")[:, HEADS * D_MODEL:2 * HEADS * D_MODEL].rearrange(
                "p (k n) -> p k n", k=HEADS)

            def bank(name, dt=F32):
                return st.enter_context(nc.psum_tensor(name, [P, 512], dt))

            pa = [bank("pa0"), bank("pa1")]
            p_seg, p_cum, p_y, p_state, p_xt, p_misc = (
                bank(n) for n in ("p_seg", "p_cum", "p_y", "p_state", "p_xt", "p_misc"))
            CB, BT = slice(0, P), slice(P, P + STATE)
            DTT = slice(192, 192 + QS * HEADS)

            ORDER = (
                "m0 x la g3- r1- t0- a0 lb v2- n1- r2- d0 t1- n2- a1 m1 v3- r3- d1 b0 lc m2 a2 g0 d2 t2- "
                "n3- s0 s1 b1 s2 s3 v0 a3 g1 r0 t3- d3 n0 p s4 b2 g2 v1 b3 m3").split()

            def late(b, first):
                return isinstance(b, int) and b >= first

            WALK_START = ["lc", *(f"s{i}" for i in range(5))]

            def uses(i, stages):
                return sum(s == "lc" or s[0] == "s" or s[0] == "vt"[i] for s in stages)

            def in_part(b):
                if late(b, BATCH):
                    return [s for s in ORDER if "-" in s]
                return [s for s in ORDER if not ((s[0] in "xlsp" or s == f"m{QS - 1}") and late(b, BATCH - 1)
                                                 or "-" in s and isinstance(b, int) and b == 0)]

            def use(i, b, stage):
                stages = in_part(b)
                here = uses(i, stages[:stages.index(stage) + 1])
                if isinstance(b, int):
                    return uses(i, WALK_START) + sum(uses(i, in_part(k)) for k in range(b)) + here
                return b * uses(i, ORDER) + (uses(i, WALK_START) + uses(i, in_part(0)) - uses(i, ORDER) + here)

            def use_s(b, n):
                if isinstance(b, int) and b == 0:
                    return n // 2 + 2
                return use(n % 2, b - 1, f"s{n // 2}")

            def use_tile(i, b, stage):
                return use(i, b + 1, stage + "-") if stage + "-" in ORDER else use(i, b, stage)

            def use_v(b, q):
                return use_tile(0, b, f"v{q}")

            def use_t(b, q):
                return use_tile(1, b, f"t{q}")

            def use_l(b, k):
                return 1 if isinstance(b, int) and b == 0 else use(k, b - 1, "lc")

            TURNED_AT = sum(s[0] == "a" for s in ORDER[:ORDER.index("s0")])
            EXP_FIRST = []
            for k, s in enumerate(ORDER):
                if s[0] in "dp" or s == "a0":
                    earlier = [t for t in ORDER[k + 1:] + ORDER[:k] if t[0] in "dps" and t != "s0" or t == "a0"]
                    if earlier[-1][0] == "s":
                        EXP_FIRST.append(s)

            def before(b, q):
                return b * QS + max(q - 1, 0)

            def walk(stages, loop):
                for s in ("x", "la", "lb", "lc"):
                    stages[s](0)
                for i in range(5):
                    stages["s"](0, 0, i)
                stages["p"](0, 0)

                def part(b, par):
                    for s in in_part(b):
                        if s[0] in "xl":
                            stages[s](b + 1)
                        elif s[0] in "sp":
                            stages[s[0]](b + 1, 1 - par, *map(int, s[1:]))
                        elif "-" in s:
                            stages[s[0]](b - 1, 1 - par, int(s[1]))
                        else:
                            stages[s[0]](b, par, int(s[1]))

                part(0, 0)
                with loop(0, BATCH // 2 - 1) as p:
                    part(p * 2 + 1, 1)
                    part(p * 2 + 2, 0)
                part(BATCH - 1, 1)
                part(BATCH, 0)

            nothing = {s: (lambda *a: None) for s in ("x", "la", "lb", "lc", "s", "p", "a", "m", "d", "b", "g", "v", "r", "n", "t")}
            CONV_ORDER = [HEADS, *range(HEADS)]
            TILE_ORDER = [("dt", 0), ("x", HEADS)]
            for m in range(HEADS):
                TILE_ORDER += [("x", m), ("z", m)]
            NT = len(TILE_ORDER)

            def tiles(i):
                return list(enumerate(TILE_ORDER))[2 * i:2 * i + 2]

            with nc.Block() as block:
                @block.sync
                def _(sp):
                    sp.dma_start(win_raw, w_in.rearrange("(k p) n -> p k n", p=P)).then_inc(sem("win_loaded"), 16)

                    def x_load(b):
                        sp.wait_ge(sem("x_normed"), b)
                        sp.dma_start(x_in[:], u_tiles(b)).then_inc(sem("x_loaded"), 16)

                    u4 = u.rearrange("b (q p) d -> b p q d", p=P)

                    def u_tiles(b):
                        return u4[b] if isinstance(b, int) else u4[bass.ds(b, 1)].rearrange("a p q d -> (a p) q d")

                    consts = [(ident[:], ident_d), (causal[:], causal_d), (later[:], later_d),
                             (small[:], small_d),
                             (rw_raw[:], gates_w.rearrange("(k p) e -> p k e", p=P))]
                    x_load(0)
                    for dst, src in consts:
                        sp.dma_start(dst, src).then_inc(sem("consts_loaded"), 16)
                    sp.dma_start(wo_raw, w_out.rearrange("(h p) n -> p h n", p=P)).then_inc(sem("wo_loaded"), 16)

                    x_tiles = u.rearrange("b (q p) d -> (b q) p d", p=P)

                    def tile_of(ap, j):
                        return ap[j] if isinstance(j, int) else ap[bass.ds(j, 1)].rearrange("a p d -> (a p) d")

                    def v(b, par, q):
                        j = b * QS + q
                        sp.wait_ge(sem(f"x1_done{q % 2}"), b * 2 + q // 2)
                        sp.dma_start(x_res[q % 2][:], tile_of(x_tiles, j)).then_inc(sem(f"res_loaded{q % 2}"), 16)

                    def r(b, par, q):
                        j = b * QS + q
                        sp.wait_ge(sem(f"x1_done{q % 2}"), b * 2 + q // 2 + 1)
                        sp.dma_start(tile_of(x1_dram, j), x1[q % 2][:]).then_inc(sem(f"x1_stored{q % 2}"), 16)

                    def x(b):
                        if not (isinstance(b, int) and b == 0):
                            x_load(b)

                    walk({**nothing, "x": x, "v": v, "r": r}, sp.Fori)
                    for i in range(2):
                        sp.wait_ge(sem(f"x1_stored{i}"), 16 * TILES // 2)

                @block.gpsimd
                def _(pool):
                    nc.gpsimd.memset(exponent[:], -0.5)
                    nc.gpsimd.memset(ones[:], 1.0).then_inc(sem("pool_consts"), 1)
                    pool.wait_ge(sem("pool_consts"), 1)

                    def la(b):
                        pool.wait_ge(sem("ve0_done"), b + 1)
                        nc.gpsimd.tensor_tensor(rs0[:], ve0[:], exponent[:], ALU.pow).then_inc(sem("rs0_done"), 1)

                    def d(b, par, q):
                        j, c = b * QS + q, q % 2
                        if q < QS - 1:
                            pool.wait_ge(sem("xs_done"), j + 1)
                            pool.wait_ge(sem("decay_done"), j + 1)
                            pool.wait_ge(sem("state_filled"), b * 3 + q)
                            nc.gpsimd.tensor_tensor(xw[:], xs[c][:], decay[c][:, :, P - 1:P].to_broadcast([P, HEADS, P]), ALU.mult).then_inc(sem("xw_done"), 1)
                        if q:
                            pool.wait_ge(sem("ce_done"), j + 1)
                            nc.gpsimd.tensor_tensor(ce[c][:], ce[c][:], c_act[par][:, q * P:(q + 1) * P].unsqueeze(1).to_broadcast([P, 2, P]), ALU.mult).then_inc(sem("ce_c_done"), 1)

                    def a(b, par, q):
                        c = q % 2
                        pool.wait_ge(sem("silu_done"), (b + 1) * XBC_TILES)
                        pool.wait_ge(sem("y_sum_done"), before(b, q))
                        nc.gpsimd.tensor_tensor(xd[c][:], xbc[par][:, 0:HEADS, q * P:(q + 1) * P], d_row.unsqueeze(2).to_broadcast([P, HEADS, P]), ALU.mult).then_inc(sem("xd_done"), 1)

                    def bb(b, par, q):
                        j, c = b * QS + q, q % 2
                        if 0 < q < QS - 1:
                            pool.wait_ge(sem("state_done"), b * 3 + q)
                            pool.wait_ge(sem("carry_done"), b + 1)
                            nc.gpsimd.tensor_tensor(state_dec[:], state[:], carry[par][:, q * 2:(q + 1) * 2].unsqueeze(2).to_broadcast([P, 2, P]), ALU.mult).then_inc(sem("state_dec_done"), 1)

                    def g(b, par, q):
                        j, c = b * QS + q, q % 2
                        pool.wait_ge(sem("yg_hi_done"), j + 1)
                        pool.wait_ge(sem("yg_done"), j + 1)
                        pool.wait_ge(sem("v_filled"), before(b, q))
                        nc.gpsimd.tensor_tensor(yg_lo[c][:], yg[:], f32(yg_hi[c][:]), ALU.subtract).then_inc(sem("yg_lo_done"), 1)
                        pool.wait_ge(sem("ysq_done"), j + 1)
                        pool.wait_ge(sem("sq_sum_done"), j)
                        nc.gpsimd.tensor_tensor(sq_pair[:], ysq[:, 0:2, :], ysq[:, 2:4, :], ALU.add).then_inc(sem("sq_pair_done"), 1)
                        pool.wait_ge(sem("sq_pair_done"), j + 1)
                        nc.gpsimd.tensor_tensor(sq_sum[c][:], sq_pair[:, 0, :], sq_pair[:, 1, :], ALU.add).then_inc(sem("sq_sum_done"), 1)

                    def v(b, par, q):
                        pool.wait_ge(sem("ve1_done"), b * QS + q + 1)
                        nc.gpsimd.tensor_tensor(rs1[:], ve1[:], exponent[:, 0:1], ALU.pow).then_inc(sem("rs1_done"), 1)

                    def r(b, par, q):
                        pool.wait_ge(sem("ve2_done"), b * QS + q + 1)
                        pool.wait_ge(sem("xn2_done"), b * QS + q)
                        nc.gpsimd.tensor_tensor(rs2[:], ve2[:], exponent[:, 0:1], ALU.pow).then_inc(sem("rs2_done"), 1)

                    walk({**nothing, "la": la, "a": a, "d": d, "b": bb, "g": g, "v": v, "r": r}, pool.Fori)

                @block.scalar
                def _(act):
                    act.wait_ge(sem("consts_loaded"), 16 * 5)
                    act.wait_ge(sem("win_loaded"), 16)
                    nc.scalar.activation(win_hi[:], win_raw, ACT.Copy).then_inc(sem("win_hi_done"), 1)
                    nc.scalar.activation(rw_hi[:], rw_raw[:], ACT.Copy).then_inc(sem("rw_hi_done"), 1)
                    nc.scalar.activation(aneg_row[:], alog_row, ACT.Exp).then_inc(sem("a_exp"), 1)
                    act.wait_ge(sem("wo_loaded"), 16)
                    for h in range(HEADS):
                        last = nc.scalar.activation(wo_scaled[:, h, :], wo_raw[:, h, :], ACT.Copy, scale=norm_col[:, h:h + 1])
                    last.then_inc(sem("wo_scaled_done"), 1)
                    act.wait_ge(sem("wo_scaled_done"), 1)
                    nc.scalar.activation(wo_hi[:], wo_scaled, ACT.Copy).then_inc(sem("wo_hi_done"), 1)

                    def lc(b):
                        for k in range(KD):
                            act.wait_ge(sem("xt_filled"), b * 2 + k + 1)
                            nc.scalar.activation(xt_hi[:, k, bass.ds(b * SEQ, SEQ)], pa[k][:], ACT.Copy).then_inc(sem("xt_hi_done"), 1)

                    def silu(b, par, o):
                        m = CONV_ORDER[o]
                        act.wait_ge(sem("conv_done"), b * XBC_TILES + o + 1)
                        src = conv_acc[o % 2]
                        if m < HEADS:
                            nc.scalar.activation(xbc[par][:, m, :], src[:], ACT.Silu).then_inc(sem("silu_done"), 1)
                        else:
                            nc.scalar.activation(xbc[par][0:STATE, m, :], src[0:STATE, :], ACT.Silu)
                            nc.scalar.activation(c_act[par][0:STATE, :], src[STATE:P, :], ACT.Silu)
                            nc.scalar.activation(c_act[par][STATE:P, :], src[STATE:P, :], ACT.Silu).then_inc(sem("silu_done"), 1)

                    def s(b, par, i):
                        if i == 0:
                            if not isinstance(b, int) or b > 1:
                                act.wait_ge(sem("y_filled"), (b - 1) * QS)
                                act.wait_ge(sem("yg_done"), (b - 1) * QS)
                            else:
                                act.wait_ge(sem("wo_lo_done"), 1)
                                act.wait_ge(sem("win_lo_done"), 1)
                        for n, (kind, m) in tiles(i):
                            act.wait_ge(sem("proj_filled"), b * NT + n + 1)
                            src = pa[n % 2]
                            free = sem(f"pa{n % 2}_free")
                            if kind == "dt":
                                if not (isinstance(b, int) and b == 0):
                                    act.wait_ge(sem("dtt_filled"), b)
                                nc.scalar.activation(dt_rows[:], src[0:HEADS, :], ACT.Copy).then_inc(free, 1)
                            elif kind == "z":
                                nc.scalar.activation(gate_z[par][:, m, :], src[:], ACT.Silu).then_inc(free, 1)
                            else:
                                o = CONV_ORDER.index(m)
                                act.wait_ge(sem("conv_done"), b * XBC_TILES + max(o - 1, 0))
                                if isinstance(b, int) and b == 0 and o == 0:
                                    act.wait_ge(sem("pads_zero"), 1)
                                nc.scalar.activation(conv_in[o % 2][:, TAPS - 1:], src[:], ACT.Copy).then_inc(sem("conv_in_done"), 1)
                                act.wait_ge(sem("silu_done"), b * XBC_TILES + max(o - 1, 0))
                                nc.scalar.activation(conv_acc[o % 2][:], src[:], ACT.Identity, bias=conv_bias[:, m:m + 1], scale=conv_taps[:, m, TAPS - 1:TAPS]).then_inc(free, 1)
                                if o:
                                    silu(b, par, o - 1)
                        if i == 4:
                            silu(b, par, XBC_TILES - 1)

                    def p(b, par):
                        if isinstance(b, int) and b == 0 or "p" in EXP_FIRST:
                            nc.scalar.preload_act_table_set("natural_log_exp_and_others")
                        act.wait_ge(sem("dt_nabs_done"), b + 1)
                        nc.scalar.activation(dt_e[:], dt_nabs[:], ACT.Exp).then_inc(sem("dt_e_done"), 1)
                        act.wait_ge(sem("dt_e_done"), b + 1)
                        nc.scalar.activation(dt_l[:], dt_e[:], ACT.Ln, bias=1.0).then_inc(sem("dt_l_done"), 1)
                        if isinstance(b, int) and b == 0:
                            steps_ahead(0, 0, 0)

                    def steps_ahead(b, par, q):
                        c = q % 2
                        act.wait_ge(sem("a_dt_done"), b + 1)
                        act.wait_ge(sem("seg_filled"), before(b, q))
                        for h in range(HEADS):
                            nc.scalar.activation(am[c][:, h, :], later[:], ACT.Copy, scale=a_dt[par][:, q * HEADS + h:q * HEADS + h + 1])
                        nc.scalar.activation(am_all[c][:], a_dt[par][:, q * HEADS:(q + 1) * HEADS].rearrange("p (h g) -> p g h", h=2).unsqueeze(3).to_broadcast([P, 2, 2, STATE]), ACT.Copy).then_inc(sem("am_done"), 1)

                    def a(b, par, q):
                        j, c = b * QS + q, q % 2
                        if f"a{q}" in EXP_FIRST:
                            nc.scalar.preload_act_table_set("natural_log_exp_and_others")
                        if q == 0:
                            act.wait_ge(sem("tot_filled"), b + 1)
                            act.wait_ge(sem("state_dec_done"), b * 2)
                            nc.scalar.activation(carry[par][:], p_state[:, 0:QS * 2], ACT.Exp).then_inc(sem("carry_done"), 1)
                        act.wait_ge(sem("cb_done"), j + 1)
                        act.wait_ge(sem("state_filled"), b * 3 + (0, 0, 1, 2)[q])
                        nc.scalar.activation(b_tok[c][:], p_misc[:, BT], ACT.Copy).then_inc(sem("b_tok_done"), 1)
                        act.wait_ge(sem("xt_tok_filled"), j + 1)
                        act.wait_ge(sem("y_filled"), before(b, q))
                        act.wait_ge(sem("xw_done"), b * 3 + (0, 0, 1, 2)[q])
                        for h in range(HEADS):
                            last = nc.scalar.activation(xs[c][:, h, :], p_xt[:, h * P:(h + 1) * P], ACT.Copy, scale=dt[par][:, q * HEADS + h:q * HEADS + h + 1])
                        last.then_inc(sem("xs_done"), 1)

                    def d(b, par, q):
                        j, c = b * QS + q, q % 2
                        if f"d{q}" in EXP_FIRST:
                            nc.scalar.preload_act_table_set("natural_log_exp_and_others")
                        act.wait_ge(sem("seg_filled"), j + 1)
                        act.wait_ge(sem("mix_done"), before(b, q))
                        nc.scalar.activation(decay[c][:].rearrange("p h l -> p (h l)"), p_seg[:], ACT.Exp).then_inc(sem("decay_done"), 1)
                        act.wait_ge(sem("ce_c_done"), b * 3 + (0, 0, 0, 1)[q])
                        act.wait_ge(sem("y_filled"), before(b, q))
                        nc.scalar.activation(ce[c][:].rearrange("p h l -> p (h l)"), p_cum[:, 0:2 * P], ACT.Exp).then_inc(sem("ce_done"), 1)

                    def m(b, par, q):
                        if q < QS - 1:
                            steps_ahead(b, par, q + 1)
                        else:
                            steps_ahead(b + 1, 1 - par, 0)

                    def g(b, par, q):
                        j, c = b * QS + q, q % 2
                        act.wait_ge(sem("yg_done"), j + 1)
                        act.wait_ge(sem("v_filled"), before(b, q))
                        act.wait_ge(sem("yg_lo_done"), before(b, q))
                        nc.scalar.activation(yg_hi[c][:], yg[:], ACT.Copy).then_inc(sem("yg_hi_done"), 1)
                        act.wait_ge(sem("sq_pair_done"), j)
                        nc.scalar.activation(ysq[:], yg[:], ACT.Square).then_inc(sem("ysq_done"), 1)

                    def t(b, par, q):
                        j = b * QS + q
                        act.wait_ge(sem("t2_filled"), j + 1)
                        nc.scalar.activation(xt_hi[:, :, bass.ds(j * P, P)], pa[1][:, 0:KD * P].rearrange("p (k n) -> p k n", k=KD), ACT.Copy).then_inc(sem("t2_hi_done"), 1)

                    walk({**nothing, "lc": lc, "s": s, "p": p, "a": a, "d": d, "m": m, "g": g, "t": t}, act.Fori)

                @block.vector
                def _(dve):
                    for i in range(2):
                        last = nc.vector.memset(conv_in[i][:, 0:TAPS - 1], 0.0)
                    last.then_inc(sem("pads_zero"), 1)

                    def setup():
                        dve.wait_ge(sem("win_hi_done"), 1)
                        nc.vector.tensor_tensor(win_lo[:], win_raw, f32(win_hi[:]), ALU.subtract).then_inc(sem("win_lo_done"), 1)
                        dve.wait_ge(sem("rw_hi_done"), 1)
                        nc.vector.tensor_tensor(rw_lo[:], rw_raw[:], f32(rw_hi[:]), ALU.subtract).then_inc(sem("rw_lo_done"), 1)
                        dve.wait_ge(sem("a_exp"), 1)
                        nc.vector.tensor_scalar(aneg_row[:], aneg_row[:], -1.0, None, ALU.mult).then_inc(sem("a_neg"), 1)
                        dve.wait_ge(sem("wo_hi_done"), 1)
                        nc.vector.tensor_tensor(wo_lo[:], wo_scaled, f32(wo_hi[:]), ALU.subtract).then_inc(sem("wo_lo_done"), 1)

                    def la(b):
                        dve.wait_ge(sem("x_loaded"), b * 16 + 16)
                        for q in range(QS):
                            last = nc.vector.bn_stats(st0[:, q, :], x_in[:, q, :])
                        last.then_inc(sem("st0_done"), 1)
                        dve.wait_ge(sem("st0_done"), b + 1)
                        hold(dve)
                        for q in range(QS):
                            last = nc.vector.bn_aggr(mv0[:, q, :], st0[:, q, :])
                        last.then_inc(sem("mv0_done"), 1)
                        dve.wait_ge(sem("mv0_done"), b + 1)
                        nc.vector.tensor_scalar(ve0[:].unsqueeze(2), mv0[:, :, 1:2], LN_EPS, None, ALU.add).then_inc(sem("ve0_done"), 1)

                    def lb(b):
                        dve.wait_ge(sem("rs0_done"), b + 1)
                        dve.wait_ge(sem("xt_filled"), b * 2)
                        for q in range(QS):
                            last = nc.vector.tensor_scalar(x_norm[:, q, :], x_in[:, q, :], mv0[:, q, 0:1], rs0[:, q:q + 1], ALU.subtract, ALU.mult)
                        last.then_inc(sem("x_normed"), 1)

                    def lc(b):
                        for k in range(KD):
                            dve.wait_ge(sem("xt_hi_done"), b * 2 + k + 1)
                            part = bass.ds(b * SEQ, SEQ)
                            nc.vector.tensor_tensor(xt_lo[:, k, part], pa[k][:], f32(xt_hi[:, k, part]), ALU.subtract).then_inc(sem(f"pa{k}_free"), 1)
                        if isinstance(b, int) and b == 0:
                            setup()

                    def step_sizes(b):
                        dve.wait_ge(sem("dtt_filled"), b + 1)
                        nc.vector.tensor_tensor(dt_y[:].rearrange("p (q h) -> p q h", h=HEADS), p_misc[:, DTT].rearrange("p (q h) -> p q h", h=HEADS), dtb_row.unsqueeze(1).to_broadcast([P, QS, HEADS]), ALU.add).then_inc(sem("dt_y_done"), 1)
                        dve.wait_ge(sem("dt_y_done"), b + 1)
                        nc.vector.tensor_scalar(dt_neg[:], dt_y[:], -1.0, None, ALU.mult).then_inc(sem("dt_neg_done"), 1)
                        dve.wait_ge(sem("dt_neg_done"), b + 1)
                        nc.vector.tensor_tensor(dt_nabs[:], dt_y[:], dt_neg[:], ALU.min).then_inc(sem("dt_nabs_done"), 1)

                    def s(b, par, i):
                        for slot, (kind, m) in tiles(i):
                            if kind != "x":
                                continue
                            o = CONV_ORDER.index(m)
                            dve.wait_ge(sem("conv_in_done"), b * XBC_TILES + o + 1)
                            dve.wait_ge(sem(f"pa{slot % 2}_free"), use_s(b, slot))
                            for k in range(TAPS - 1):
                                last = nc.vector.scalar_tensor_tensor(conv_acc[o % 2][:], conv_in[o % 2][:, k:k + SEQ], conv_taps[:, m, k:k + 1], conv_acc[o % 2][:], ALU.mult, ALU.add)
                                if k < TAPS - 2:
                                    last.then_inc(sem("tap_done"), 1)
                                    dve.wait_ge(sem("tap_done"), (b * XBC_TILES + o) * (TAPS - 2) + k + 1)
                            last.then_inc(sem("conv_done"), 1)
                            if o == 0:
                                step_sizes(b)

                    def p(b, par):
                        dve.wait_ge(sem("dt_l_done"), b + 1)
                        nc.vector.scalar_tensor_tensor(dt[par][:], dt_y[:], 0.0, dt_l[:], ALU.max, ALU.add).then_inc(sem("dt_done"), 1)
                        dve.wait_ge(sem("dt_done"), b + 1)
                        nc.vector.tensor_tensor(a_dt[par][:].rearrange("p (q h) -> p q h", h=HEADS), dt[par][:].rearrange("p (q h) -> p q h", h=HEADS), aneg_row[:].unsqueeze(1).to_broadcast([P, QS, HEADS]), ALU.mult).then_inc(sem("a_dt_done"), 1)

                    def a(b, par, q):
                        j, c = b * QS + q, q % 2
                        dve.wait_ge(sem("misc_filled"), j + 1)
                        dve.wait_ge(sem("mix_done"), before(b, q))
                        nc.vector.tensor_tensor(cb[c][:], p_misc[:, CB], causal[:], ALU.mult).then_inc(sem("cb_done"), 1)

                    def d(b, par, q):
                        j, c = b * QS + q, q % 2
                        dve.wait_ge(sem("cb_done"), j + 1)
                        dve.wait_ge(sem("decay_done"), j + 1)
                        dve.wait_ge(sem("y_filled"), before(b, q))
                        nc.vector.tensor_tensor(mix[c][:], decay[c][:], cb[c][:].unsqueeze(1).to_broadcast([P, HEADS, P]), ALU.mult).then_inc(sem("mix_done"), 1)

                    def bb(b, par, q):
                        j, c = b * QS + q, q % 2
                        if q < QS - 1:
                            dve.wait_ge(sem("state_filled"), b * 3 + q + 1)
                            if q:
                                dve.wait_ge(sem("state_dec_done"), b * 2 + q)
                                nc.vector.tensor_tensor(state[:], state_dec[:], p_state[:, 0:2 * P].rearrange("p (h l) -> p h l", h=2), ALU.add).then_inc(sem("state_done"), 1)
                            else:
                                nc.vector.tensor_copy(state[:], p_state[:, 0:2 * P].rearrange("p (h l) -> p h l", h=2)).then_inc(sem("state_done"), 1)

                    def g(b, par, q):
                        j, c = b * QS + q, q % 2
                        dve.wait_ge(sem("y_filled"), j + 1)
                        dve.wait_ge(sem("yg_done"), j)
                        dve.wait_ge(sem("xd_done"), j + 1)
                        nc.vector.tensor_tensor(y_sum[:], xd[c][:], p_y[:].rearrange("p (h l) -> p h l", h=HEADS), ALU.add).then_inc(sem("y_sum_done"), 1)
                        dve.wait_ge(sem("y_sum_done"), j + 1)
                        dve.wait_ge(sem("yg_lo_done"), j)
                        dve.wait_ge(sem("ysq_done"), j)
                        nc.vector.tensor_tensor(yg[:], y_sum[:], gate_z[par][:, :, q * P:(q + 1) * P], ALU.mult).then_inc(sem("yg_done"), 1)

                    def v(b, par, q):
                        j = b * QS + q
                        dve.wait_ge(sem("v_filled"), j + 1)
                        nc.vector.bn_stats(st1[:], pa[0][:, 0:D_MODEL]).then_inc(sem("st1_done"), 1)
                        nc.vector.tensor_scalar(sse[:], pa[0][:, D_MODEL:D_MODEL + 1], 1.0 / D_INNER, LN_EPS, ALU.mult, ALU.add).then_inc(sem("sse_done"), 1)
                        dve.wait_ge(sem("st1_done"), j + 1)
                        hold(dve)
                        nc.vector.bn_aggr(mv1[:], st1[:]).then_inc(sem("mv1_done"), 1)
                        dve.wait_ge(sem("mv1_done"), j + 1)
                        dve.wait_ge(sem("sse_done"), j + 1)
                        nc.vector.scalar_tensor_tensor(ve1[:], sse[:], LN_EPS, mv1[:, 1:2], ALU.mult, ALU.add).then_inc(sem("ve1_done"), 1)

                    def r(b, par, q):
                        j, c = b * QS + q, q % 2
                        dve.wait_ge(sem("rs1_done"), j + 1)
                        nc.vector.tensor_scalar(shifted[:], pa[0][:, 0:D_MODEL], mv1[:, 0:1], rs1[:], ALU.subtract, ALU.mult).then_inc(sem("pa0_free"), 1)
                        dve.wait_ge(sem("pa0_free"), use_v(b, q))
                        dve.wait_ge(sem(f"res_loaded{c}"), (b * 2 + q // 2) * 16 + 16)
                        dve.wait_ge(sem(f"x1_stored{c}"), (b * 2 + q // 2) * 16)
                        dve.wait_ge(sem("xn2_done"), j)
                        nc.vector.tensor_tensor(x1[c][:], x_res[c][:], shifted[:], ALU.add).then_inc(sem(f"x1_done{c}"), 1)
                        dve.wait_ge(sem(f"x1_done{c}"), b * 2 + q // 2 + 1)
                        nc.vector.bn_stats(st2[:], x1[c][:]).then_inc(sem("st2_done"), 1)
                        dve.wait_ge(sem("st2_done"), j + 1)
                        hold(dve)
                        nc.vector.bn_aggr(mv2[:], st2[:]).then_inc(sem("mv2_done"), 1)
                        dve.wait_ge(sem("mv2_done"), j + 1)
                        nc.vector.tensor_scalar(ve2[:], mv2[:, 1:2], LN_EPS, None, ALU.add).then_inc(sem("ve2_done"), 1)

                    def n(b, par, q):
                        j, c = b * QS + q, q % 2
                        dve.wait_ge(sem("rs2_done"), j + 1)
                        dve.wait_ge(sem("t2_filled"), j)
                        nc.vector.tensor_scalar(xn2[:], x1[c][:], mv2[:, 0:1], rs2[:], ALU.subtract, ALU.mult).then_inc(sem("xn2_done"), 1)

                    def t(b, par, q):
                        j = b * QS + q
                        dve.wait_ge(sem("t2_hi_done"), j + 1)
                        part = bass.ds(j * P, P)
                        nc.vector.tensor_tensor(xt_lo[:, :, part], pa[1][:, 0:KD * P].rearrange("p (k n) -> p k n", k=KD), f32(xt_hi[:, :, part]), ALU.subtract).then_inc(sem("pa1_free"), 1)

                    walk({**nothing, "la": la, "lb": lb, "lc": lc, "s": s, "p": p, "a": a, "d": d, "b": bb, "g": g, "v": v, "r": r, "n": n, "t": t}, dve.Fori)

                @block.tensor
                def _(pe):
                    pe.wait_ge(sem("consts_loaded"), 16 * 5)
                    pe.wait_ge(sem("pool_consts"), 1)

                    def three(out, lh, ll, rh, rl, start, stop):
                        nc.tensor.matmul(out, lh, rh, start=start, stop=False)
                        nc.tensor.matmul(out, lh, rl, start=False, stop=False)
                        return nc.tensor.matmul(out, ll, rh, start=False, stop=stop)

                    def lc(b):
                        pe.wait_ge(sem("x_normed"), b + 1)
                        for k in range(KD):
                            pe.wait_ge(sem(f"pa{k}_free"), use_l(b, k) - 1)
                            for q in range(QS):
                                last = nc.tensor.transpose(pa[k][:, q * P:(q + 1) * P], x_norm[:, q, k * P:(k + 1) * P], ident[:])
                            last.then_inc(sem("xt_filled"), 1)

                    def turn_steps(b):
                        pe.wait_ge(sem("pa0_free"), use_s(b, 0))
                        if not (isinstance(b, int) and b == 0):
                            pe.wait_ge(sem("cb_done"), (b - 1) * QS + TURNED_AT)
                            pe.wait_ge(sem("b_tok_done"), (b - 1) * QS + TURNED_AT)
                        hold(pe)
                        for q in range(QS):
                            last = nc.tensor.transpose(p_misc[:, 192 + q * HEADS:192 + (q + 1) * HEADS], dt_rows[:, q * P:(q + 1) * P], ident[0:HEADS, 0:HEADS])
                        last.then_inc(sem("dtt_filled"), 1)

                    def s(b, par, i):
                        if isinstance(b, int) and b == 0:
                            pe.wait_ge(sem("win_lo_done"), 1)
                        if i == 0:
                            for k in range(KD):
                                pe.wait_ge(sem(f"pa{k}_free"), use_l(b, k))
                        for n, (kind, m) in tiles(i):
                            pe.wait_ge(sem(f"pa{n % 2}_free"), use_s(b, n) - 1)
                            if kind == "dt":
                                c0, w = DT_COL, HEADS
                            elif kind == "z":
                                c0, w = m * P, P
                            else:
                                c0, w = D_INNER + m * P, P
                            for k in range(KD):
                                part = bass.ds(b * SEQ, SEQ)
                                last = three(pa[n % 2][0:w, :], win_hi[:, k, c0:c0 + w], win_lo[:, k, c0:c0 + w],
                                             xt_hi[:, k, part], xt_lo[:, k, part], k == 0, k == KD - 1)
                            last.then_inc(sem("proj_filled"), 1)
                            if n == 1:
                                turn_steps(b)

                    def a(b, par, q):
                        j, c = b * QS + q, q % 2
                        ts = slice(q * P, (q + 1) * P)
                        if q == TURNED_AT and not late(b, BATCH - 1):
                            pe.wait_ge(sem("dt_y_done"), b + 2)
                        if q == 0:
                            pe.wait_ge(sem("dt_y_done"), b + 1)
                            pe.wait_ge(sem("silu_done"), (b + 1) * XBC_TILES)
                            pe.wait_ge(sem("a_dt_done"), b + 1)
                        pe.wait_ge(sem("cb_done"), j)
                        pe.wait_ge(sem("b_tok_done"), j)
                        if q == 0:
                            pe.wait_ge(sem("state_done"), b * 3)
                            totals = a_dt[par][:].rearrange("p (q h g) -> p h q g", h=2, g=2)
                            for half in range(2):
                                last = nc.tensor.matmul(p_state[half * STATE:(half + 1) * STATE, 0:QS * 2], ones[:, 0:STATE], totals[:, half], start=True, stop=True)
                            last.then_inc(sem("tot_filled"), 1)
                        nc.tensor.matmul(p_misc[:, CB], xbc[par][0:STATE, HEADS, ts], c_act[par][0:STATE, ts], start=True, stop=True)
                        nc.tensor.transpose(p_misc[:, BT], xbc[par][0:STATE, HEADS, ts], ident[0:STATE, 0:STATE]).then_inc(sem("misc_filled"), 1)
                        pe.wait_ge(sem("xs_done"), j)
                        for h in range(HEADS):
                            last = nc.tensor.transpose(p_xt[:, h * P:(h + 1) * P], xbc[par][:, h, ts], ident[:])
                        last.then_inc(sem("xt_tok_filled"), 1)

                    def d(b, par, q):
                        j, c = b * QS + q, q % 2
                        pe.wait_ge(sem("am_done"), j + 1)
                        pe.wait_ge(sem("decay_done"), j)
                        pe.wait_ge(sem("ce_done"), j)
                        for h in range(HEADS):
                            nc.tensor.matmul(p_seg[:, h * P:(h + 1) * P], am[c][:, h, :], causal[:], start=True, stop=True)
                        for g in range(2):
                            last = nc.tensor.matmul(p_cum[:, g * P:(g + 1) * P], am_all[c][:, g].rearrange("p h n -> p (h n)"), causal[:], start=True, stop=True)
                        last.then_inc(sem("seg_filled"), 1)

                    def bb(b, par, q):
                        j, c = b * QS + q, q % 2
                        pe.wait_ge(sem("xs_done"), j + 1)
                        pe.wait_ge(sem("mix_done"), j + 1)
                        pe.wait_ge(sem("y_sum_done"), j)
                        if q:
                            pe.wait_ge(sem("ce_c_done"), b * 3 + q)
                            pe.wait_ge(sem("state_done"), b * 3 + q)
                        def inside(h):
                            return nc.tensor.matmul(p_y[:, h * P:(h + 1) * P], xs[c][:, h, :], mix[c][:, h, :], start=(h == 0), stop=(q == 0), skip_group_check=True)

                        def carried(h):
                            rows = slice(h // 2 * STATE, (h // 2 + 1) * STATE)
                            return nc.tensor.matmul(p_y[:, h * P:(h + 1) * P], state[rows, h % 2, :], ce[c][rows, h % 2, :], start=False, stop=True, skip_group_check=True)

                        inside(0)
                        inside(1)
                        if q:
                            carried(0)
                            carried(1).then_inc(sem("lower_rows_done"), 1)
                        inside(2)
                        last = inside(3)
                        if q:
                            pe.wait_ge(sem("lower_rows_done"), b * 3 + q)
                            carried(2)
                            last = carried(3)
                        last.then_inc(sem("y_filled"), 1)
                        if q < QS - 1:
                            pe.wait_ge(sem("xw_done"), b * 3 + q + 1)
                            pe.wait_ge(sem("b_tok_done"), j + 1)
                            pe.wait_ge(sem("state_done"), b * 3 + q)
                            if q == 0:
                                pe.wait_ge(sem("carry_done"), b + 1)
                            for half in range(2):
                                last = nc.tensor.matmul(p_state[half * STATE:(half + 1) * STATE, 0:2 * P], b_tok[c][:], xw[:, 2 * half:2 * half + 2, :].rearrange("p h l -> p (h l)"), start=True, stop=True)
                            last.then_inc(sem("state_filled"), 1)

                    def v(b, par, q):
                        j, c = b * QS + q, q % 2
                        if isinstance(b, int) and b == 0 and q == 0:
                            pe.wait_ge(sem("wo_lo_done"), 1)
                        pe.wait_ge(sem("pa0_free"), use_v(b, q) - 1)
                        pe.wait_ge(sem("sq_sum_done"), j + 1)
                        pe.wait_ge(sem("yg_lo_done"), j + 1)
                        nc.tensor.matmul(pa[0][:, D_MODEL:D_MODEL + 1], sq_sum[c][:], ones[:, 0:1], start=True, stop=True)
                        for h in range(HEADS):
                            last = three(pa[0][:, 0:D_MODEL], yg_hi[c][:, h, :], yg_lo[c][:, h, :], wo_hi[:, h, :], wo_lo[:, h, :], h == 0, h == HEADS - 1)
                        last.then_inc(sem("v_filled"), 1)

                    def t(b, par, q):
                        j = b * QS + q
                        pe.wait_ge(sem("xn2_done"), j + 1)
                        pe.wait_ge(sem("pa1_free"), use_t(b, q) - 1)
                        for k in range(KD):
                            last = nc.tensor.transpose(pa[1][:, k * P:(k + 1) * P], xn2[:, k * P:(k + 1) * P], ident[:])
                        last.then_inc(sem("t2_filled"), 1)

                    walk({**nothing, "lc": lc, "s": s, "a": a, "d": d, "b": bb, "v": v, "t": t}, pe.Fori)

        with ExitStack() as st:
            comb_t = alloc(st, "comb_t", [PARTS * GATES, TOKENS], BF16)
            spread = alloc(st, "spread", [PARTS * GATES, CHUNKS, P], BF16)
            ident_b = alloc(st, "ident_b", [P, P], BF16)
            acc = alloc(st, "acc", [P, TILES, D_MODEL])

            with ExitStack() as rt:
                logit_rows = [alloc(rt, f"logit_rows{i}", [GATES, SEQ]) for i in range(2)]
                logits = alloc(rt, "logits", [P, TILES, GATES])
                index = alloc(rt, "index", [P, EXPERTS])
                top = alloc(rt, "top", [P, TILES])
                shifted2 = alloc(rt, "shifted2", [P, TILES, EXPERTS])
                expd = alloc(rt, "expd", [P, TILES, EXPERTS])
                total = alloc(rt, "total", [P, TILES])
                rtotal = alloc(rt, "rtotal", [P, TILES])
                probs = alloc(rt, "probs", [P, TILES, EXPERTS])
                top8 = alloc(rt, "top8", [P, TILES, 8])
                idx8 = alloc(rt, "idx8", [P, TILES, 8], U32)
                idxf = alloc(rt, "idxf", [P, TILES, 8])
                hit = [alloc(rt, f"hit{i}", [P, TILES, EXPERTS]) for i in range(TOP_K)]
                kept = alloc(rt, "kept", [P, TILES])
                kept_c = alloc(rt, "kept_c", [P, TILES])
                rkept = alloc(rt, "rkept", [P, TILES])
                chosen = alloc(rt, "chosen", [P, TILES, EXPERTS])
                sg_e = alloc(rt, "sg_e", [P, TILES])
                sg_1 = alloc(rt, "sg_1", [P, TILES])
                comb = alloc(rt, "comb", [P, TILES, GATES])
                rest = [alloc(rt, f"rest{i}", [P, TILES, GATES]) for i in range(2)]
                parts = alloc(rt, "parts", [P, TILES, PARTS * GATES], BF16)
                p_logit = [rt.enter_context(nc.psum_tensor(f"p_logit{i}", [P, 512], F32)) for i in range(2)]
                p_tok = [rt.enter_context(nc.psum_tensor(f"p_tok{i}", [P, 512], F32)) for i in range(2)]
                p_comb = [rt.enter_context(nc.psum_tensor(f"p_comb{i}", [P, 1024], BF16)) for i in range(2)]
                CT = 8

                with nc.Block() as block:
                    @block.sync
                    def _(sp):
                        for dst, src in ((index[:], index_d), (spread[:], spread_d.bitcast(BF16))):
                            sp.dma_start(dst, src).then_inc(sem("router_consts"), 16)

                    @block.scalar
                    def _(act):
                        with act.Fori(0, BATCH // 2) as p:
                            for i in range(2):
                                act.wait_ge(sem(f"logit_filled{i}"), p + 1)
                                act.wait_ge(sem(f"logit_turned{i}"), p)
                                nc.scalar.activation(logit_rows[i][:], p_logit[i][0:GATES, :], ACT.Copy).then_inc(sem(f"logit_rows_done{i}"), 1)
                        act.wait_ge(sem("shifted2_done"), 1)
                        nc.scalar.activation(expd[:], shifted2[:], ACT.Exp)
                        nc.scalar.activation(sg_e[:].unsqueeze(2), logits[:, :, EXPERTS:], ACT.Exp, scale=-1.0).then_inc(sem("exps_done"), 1)
                        for r in range(TILES // CT):
                            act.wait_ge(sem("comb_turned"), r + 1)
                            nc.scalar.activation(comb_t[:, r * CT * P:(r + 1) * CT * P], p_comb[r % 2][0:PARTS * GATES, :], ACT.Copy).then_inc(sem("comb_t_done"), 1)

                    @block.vector
                    def _(dve):
                        steps = [0]

                        def then(ins):
                            steps[0] += 1
                            ins.then_inc(sem("router_step"), 1)
                            dve.wait_ge(sem("router_step"), steps[0])

                        def wide(ap, n):
                            return ap.unsqueeze(2).to_broadcast([P, TILES, n])

                        nc.vector.tensor_copy(ident_b[:], ident[:]).then_inc(sem("ident_b_done"), 1)
                        with dve.Fori(0, BATCH // 2) as p:
                            for i in range(2):
                                dve.wait_ge(sem(f"logit_turned{i}"), p + 1)
                                nc.vector.tensor_copy(logits[:, bass.ds((p * 2 + i) * QS, QS), :], p_tok[i][:, 0:QS * GATES].rearrange("p (q e) -> p q e", q=QS)).then_inc(sem(f"logits_done{i}"), 1)
                        for i in range(2):
                            dve.wait_ge(sem(f"logits_done{i}"), BATCH // 2)
                        then(nc.vector.tensor_reduce(top[:], logits[:, :, 0:EXPERTS], AX.X, ALU.max))
                        nc.vector.tensor_tensor(shifted2[:], logits[:, :, 0:EXPERTS], wide(top[:], EXPERTS), ALU.subtract).then_inc(sem("shifted2_done"), 1)
                        dve.wait_ge(sem("exps_done"), 1)
                        then(nc.vector.tensor_reduce(total[:], expd[:], AX.X, ALU.add))
                        then(nc.vector.reciprocal(rtotal[:], total[:]))
                        then(nc.vector.tensor_tensor(probs[:], expd[:], wide(rtotal[:], EXPERTS), ALU.mult))
                        for t in range(TILES):
                            last = nc.vector.max(top8[:, t, :], probs[:, t, :])
                        then(last)
                        for t in range(TILES):
                            last = nc.vector.max_index(idx8[:, t, :], top8[:, t, :], probs[:, t, :])
                        then(last)
                        then(nc.vector.tensor_copy(idxf[:], idx8[:]))
                        dve.wait_ge(sem("router_consts"), 32)
                        for k in range(TOP_K):
                            last = nc.vector.tensor_tensor(hit[k][:], index[:].unsqueeze(1).to_broadcast([P, TILES, EXPERTS]), wide(idxf[:, :, k], EXPERTS), ALU.is_equal)
                        then(last)
                        nc.vector.tensor_tensor(hit[0][:], hit[0][:], hit[1][:], ALU.add)
                        then(nc.vector.tensor_tensor(hit[2][:], hit[2][:], hit[3][:], ALU.add))
                        then(nc.vector.tensor_tensor(hit[1][:], hit[0][:], hit[2][:], ALU.add))
                        then(nc.vector.tensor_tensor(chosen[:], probs[:], hit[1][:], ALU.mult))
                        then(nc.vector.tensor_reduce(kept[:], top8[:, :, 0:TOP_K], AX.X, ALU.add))
                        then(nc.vector.tensor_scalar(kept_c[:], kept[:], 1e-9, None, ALU.max))
                        then(nc.vector.reciprocal(rkept[:], kept_c[:]))
                        nc.vector.tensor_tensor(comb[:, :, 0:EXPERTS], chosen[:], wide(rkept[:], EXPERTS), ALU.mult)
                        then(nc.vector.tensor_scalar(sg_1[:], sg_e[:], 1.0, None, ALU.add))
                        then(nc.vector.reciprocal(comb[:, :, EXPERTS:], sg_1[:].unsqueeze(2)))
                        then(nc.vector.tensor_copy(parts[:, :, 0:GATES], comb[:]))
                        then(nc.vector.tensor_tensor(rest[0][:], comb[:], parts[:, :, 0:GATES], ALU.subtract))
                        then(nc.vector.tensor_copy(parts[:, :, GATES:2 * GATES], rest[0][:]))
                        then(nc.vector.tensor_tensor(rest[1][:], rest[0][:], parts[:, :, GATES:2 * GATES], ALU.subtract))
                        nc.vector.tensor_copy(parts[:, :, 2 * GATES:], rest[1][:]).then_inc(sem("parts_done"), 1)

                    @block.gpsimd
                    def _(pool):
                        nc.gpsimd.memset(acc[:], 0.0).then_inc(sem("acc_zero"), 1)

                    @block.tensor
                    def _(pe):
                        def logit_cols(p, i):
                            part = bass.ds((p * 2 + i) * SEQ, SEQ)
                            for k in range(KD):
                                nc.tensor.matmul(p_logit[i][0:GATES, :], rw_hi[:, k, :], xt_hi[:, k, part], start=(k == 0), stop=False)
                                nc.tensor.matmul(p_logit[i][0:GATES, :], rw_hi[:, k, :], xt_lo[:, k, part], start=False, stop=False)
                                last = nc.tensor.matmul(p_logit[i][0:GATES, :], rw_lo[:, k, :], xt_hi[:, k, part], start=False, stop=(k == KD - 1))
                            last.then_inc(sem(f"logit_filled{i}"), 1)

                        with pe.Fori(0, BATCH // 2) as p:
                            for i in range(2):
                                pe.wait_ge(sem(f"logit_rows_done{i}"), p)
                                logit_cols(p, i)
                            for i in range(2):
                                pe.wait_ge(sem(f"logit_rows_done{i}"), p + 1)
                                pe.wait_ge(sem(f"logits_done{i}"), p)
                                hold(pe)
                                for q in range(QS):
                                    last = nc.tensor.transpose(p_tok[i][:, q * GATES:(q + 1) * GATES], logit_rows[i][:, q * P:(q + 1) * P], ident[0:GATES, 0:GATES])
                                last.then_inc(sem(f"logit_turned{i}"), 1)
                        pe.wait_ge(sem("ident_b_done"), 1)
                        pe.wait_ge(sem("parts_done"), 1)
                        for r in range(TILES // CT):
                            if r >= 2:
                                pe.wait_ge(sem("comb_t_done"), r - 1)
                            for t in range(CT):
                                last = nc.tensor.transpose(p_comb[r % 2][0:PARTS * GATES, t * P:(t + 1) * P], parts[:, r * CT + t, :], ident_b[:])
                            last.then_inc(sem("comb_turned"), 1)

            with ExitStack() as mo:
                raw = [alloc(mo, f"raw{c}", [P, W_COLS]) for c in range(GROUP)]
                w_hi = [[alloc(mo, f"w_hi{h}{c}", [P, W_COLS], F32R) for c in range(GROUP)] for h in range(2)]
                w_lo = [[alloc(mo, f"w_lo{h}{c}", [P, W_COLS], F32R) for c in range(GROUP)] for h in range(2)]
                silu_g = [alloc(mo, f"silu_g{c}", [P, SEQ]) for c in range(GROUP)]
                weighted = [alloc(mo, f"weighted{c}", [P, SEQ]) for c in range(GROUP)]
                hidden = [alloc(mo, f"hidden{c}", [P, SEQ]) for c in range(GROUP)]
                h_hi = [alloc(mo, f"h_hi{c}", [P, SEQ], F32R) for c in range(GROUP)]
                h_lo = [alloc(mo, f"h_lo{c}", [P, SEQ], F32R) for c in range(GROUP)]
                partial = alloc(mo, "partial", [P, QS, D_MODEL])

                def mbank(name, n=512):
                    return mo.enter_context(nc.psum_tensor(name, [P, n], F32))

                p_g = [mbank(f"p_g{c}") for c in range(GROUP)]
                p_c = [mbank(f"p_c{c}") for c in range(GROUP)]
                p_u = [mbank(f"p_u{c}") for c in range(GROUP)]
                p_out = [mbank(f"p_out{i}") for i in range(2)]

                def walk_experts(stages, loop):
                    prep, up, down = stages["prep"], stages["up"], stages["down"]

                    def step(g, half, t, ahead):
                        up(g, half, t, 1)
                        down(g, half, t, 0)
                        if ahead:
                            up(*ahead, 0)
                        down(g, half, t, 1)

                    def pair(pp, final):
                        for half in range(2):
                            g = pp * 2 + half
                            more = not (final and half)
                            if more:
                                prep(g + 1, 1 - half, pp + half)
                            with loop(0, BATCH - 1) as t:
                                step(g, half, t, (g, half, t + 1))
                            step(g, half, BATCH - 1, (g + 1, 1 - half, 0) if more else None)

                    prep(0, 0, 0)
                    up(0, 0, 0, 0)
                    with loop(0, GROUPS // 2 - 1) as pp:
                        pair(pp, False)
                    pair(GROUPS // 2 - 1, True)

                idle = {"prep": lambda *a: None, "up": lambda *a: None, "down": lambda *a: None}

                with nc.Block() as block:
                    @block.sync
                    def _(sp):
                        with sp.Fori(0, GROUPS) as g:
                            for c in range(GROUP):
                                sp.wait_ge(sem(f"w_ready{c}"), g)
                                sp.dma_start(raw[c][:], moe_w[bass.ds(g * GROUP + c, 1)].rearrange("a p n -> (a p) n")).then_inc(sem(f"raw_loaded{c}"), 16)

                    @block.scalar
                    def _(act):
                        def prep(g, half, uses):
                            act.wait_ge(sem(f"group_done{half}"), uses)
                            for c in range(GROUP):
                                act.wait_ge(sem(f"raw_loaded{c}"), g * 16 + 16)
                                nc.scalar.activation(w_hi[half][c][:], raw[c][:], ACT.Copy).then_inc(sem(f"w_hi_done{c}"), 1)

                        def up(g, half, t, c):
                            i = g * BATCH + t
                            act.wait_ge(sem(f"g_filled{c}"), i + 1)
                            act.wait_ge(sem(f"weighted_done{c}"), i)
                            nc.scalar.activation(silu_g[c][:], p_g[c][:], ACT.Silu).then_inc(sem(f"silu_g_done{c}"), 1)

                        def down(g, half, t, c):
                            if c == 0:
                                return
                            i = g * BATCH + t
                            act.wait_ge(sem("down_done1"), i + 1)
                            act.wait_ge(sem("acc_done"), i)
                            for o in range(2):
                                last = nc.scalar.activation(partial[:, 2 * o:2 * o + 2, :], p_out[o][:].rearrange("p (q n) -> p q n", q=2), ACT.Copy)
                            last.then_inc(sem("partial_done"), 1)

                        walk_experts({"prep": prep, "up": up, "down": down}, act.Fori)

                    @block.gpsimd
                    def _(pool):
                        def prep(g, half, uses):
                            for c in range(GROUP):
                                pool.wait_ge(sem(f"w_hi_done{c}"), g + 1)
                                nc.gpsimd.tensor_tensor(w_lo[half][c][:], raw[c][:], f32(w_hi[half][c][:]), ALU.subtract).then_inc(sem(f"w_ready{c}"), 1)

                        def down(g, half, t, c):
                            if c == 0:
                                return
                            i = g * BATCH + t
                            pool.wait_ge(sem("partial_done"), i + 1)
                            part = acc[:, bass.ds(t * QS, QS), :]
                            nc.gpsimd.tensor_tensor(part, part, partial[:], ALU.add).then_inc(sem("acc_done"), 1)

                        walk_experts({**idle, "prep": prep, "down": down}, pool.Fori)

                    @block.vector
                    def _(dve):
                        def up(g, half, t, c):
                            i = g * BATCH + t
                            dve.wait_ge(sem(f"silu_g_done{c}"), i + 1)
                            dve.wait_ge(sem(f"c_filled{c}"), i + 1)
                            nc.vector.tensor_tensor(weighted[c][:], silu_g[c][:], p_c[c][:], ALU.mult).then_inc(sem(f"weighted_done{c}"), 1)
                            dve.wait_ge(sem(f"weighted_done{c}"), i + 1)
                            dve.wait_ge(sem(f"u_filled{c}"), i + 1)
                            nc.vector.tensor_tensor(hidden[c][:], weighted[c][:], p_u[c][:], ALU.mult).then_inc(sem(f"hidden_done{c}"), 1)
                            dve.wait_ge(sem(f"hidden_done{c}"), i + 1)
                            dve.wait_ge(sem(f"down_done{c}"), i)
                            nc.vector.tensor_copy(h_hi[c][:], hidden[c][:]).then_inc(sem(f"h_hi_done{c}"), 1)
                            dve.wait_ge(sem(f"h_hi_done{c}"), i + 1)
                            nc.vector.tensor_tensor(h_lo[c][:], hidden[c][:], f32(h_hi[c][:]), ALU.subtract).then_inc(sem(f"h_lo_done{c}"), 1)

                        walk_experts({**idle, "up": up}, dve.Fori)

                    @block.tensor
                    def _(pe):
                        def up(g, half, t, c):
                            i = g * BATCH + t
                            part = bass.ds(t * SEQ, SEQ)
                            chunk_g = g * GROUP + c
                            pe.wait_ge(sem(f"w_ready{c}"), g + 1)

                            def project(bank, off):
                                for k in range(KD):
                                    cols = slice(off + k * P, off + (k + 1) * P)
                                    hi, lo = w_hi[half][c][:, cols], w_lo[half][c][:, cols]
                                    nc.tensor.matmul(bank[:], hi, xt_hi[:, k, part], start=(k == 0), stop=False)
                                    nc.tensor.matmul(bank[:], hi, xt_lo[:, k, part], start=False, stop=False)
                                    last = nc.tensor.matmul(bank[:], lo, xt_hi[:, k, part], start=False, stop=(k == KD - 1))
                                return last

                            pe.wait_ge(sem(f"silu_g_done{c}"), i)
                            project(p_g[c], G_OFF).then_inc(sem(f"g_filled{c}"), 1)
                            pe.wait_ge(sem(f"weighted_done{c}"), i)
                            nc.tensor.matmul(p_c[c][:], spread[:, bass.ds(chunk_g, 1), :].rearrange("r a p -> r (a p)"), comb_t[:, part], start=True, stop=True).then_inc(sem(f"c_filled{c}"), 1)
                            pe.wait_ge(sem(f"hidden_done{c}"), i)
                            project(p_u[c], U_OFF).then_inc(sem(f"u_filled{c}"), 1)

                        def down(g, half, t, c):
                            i = g * BATCH + t
                            pe.wait_ge(sem(f"h_hi_done{c}"), i + 1)
                            if c == 0:
                                pe.wait_ge(sem("partial_done"), i)
                            wd_hi, wd_lo = w_hi[half][c][:, D_OFF:], w_lo[half][c][:, D_OFF:]

                            def out(q):
                                return p_out[q // 2][:, (q % 2) * D_MODEL:(q % 2 + 1) * D_MODEL]

                            for q in range(QS):
                                cols = slice(q * P, (q + 1) * P)
                                nc.tensor.matmul(out(q), h_hi[c][:, cols], wd_hi, start=(c == 0 and q % 2 == 0), stop=False, skip_group_check=True)
                                nc.tensor.matmul(out(q), h_hi[c][:, cols], wd_lo, start=False, stop=False, skip_group_check=True)
                            pe.wait_ge(sem(f"h_lo_done{c}"), i + 1)
                            for q in range(QS):
                                last = nc.tensor.matmul(out(q), h_lo[c][:, q * P:(q + 1) * P], wd_hi, start=False, stop=(c == GROUP - 1), skip_group_check=True)
                            last.then_inc(sem(f"down_done{c}"), 1)
                            if c == GROUP - 1 and isinstance(t, int):
                                pe.wait_ge(sem(f"down_done{c}"), i + 1)
                                pe.sem_inc(sem(f"group_done{half}"), 1)

                        walk_experts({**idle, "up": up, "down": down}, pe.Fori)

            with ExitStack() as fi:
                x1_in = [alloc(fi, f"x1_in{i}", [P, QS, D_MODEL]) for i in range(2)]
                normed = [alloc(fi, f"normed{i}", [P, QS, D_MODEL]) for i in range(2)]
                final = [alloc(fi, f"final{i}", [P, QS, D_MODEL]) for i in range(2)]
                stf = [alloc(fi, f"stf{i}", [P, QS, 6]) for i in range(2)]
                mvf = [alloc(fi, f"mvf{i}", [P, QS, 2]) for i in range(2)]
                vef = [alloc(fi, f"vef{i}", [P, QS]) for i in range(2)]
                rsf = [alloc(fi, f"rsf{i}", [P, QS]) for i in range(2)]
                x1_v = x1_dram.rearrange("(b q) p d -> b p q d", q=QS)
                out_v = out.rearrange("b (q p) d -> b p q d", p=P)
                with nc.Block() as block:
                    @block.sync
                    def _(sp):
                        with sp.Fori(0, BATCH // 2) as p:
                            for i in range(2):
                                sp.wait_ge(sem(f"final_done{i}"), p)
                                sp.dma_start(x1_in[i][:], x1_v[bass.ds(p * 2 + i, 1)].rearrange("a p q d -> (a p) q d")).then_inc(sem(f"x1_back{i}"), 16)

                    @block.scalar
                    def _(act):
                        with act.Fori(0, BATCH // 2) as p:
                            for i in range(2):
                                act.wait_ge(sem(f"final_done{i}"), p + 1)
                                act.dma_start(out_v[bass.ds(p * 2 + i, 1)].rearrange("a p q d -> (a p) q d"), final[i][:]).then_inc(sem(f"out_stored{i}"), 16)
                        for i in range(2):
                            act.wait_ge(sem(f"out_stored{i}"), 16 * (BATCH // 2))

                    @block.gpsimd
                    def _(pool):
                        with pool.Fori(0, BATCH // 2) as p:
                            for i in range(2):
                                pool.wait_ge(sem(f"vef_done{i}"), p + 1)
                                nc.gpsimd.tensor_tensor(rsf[i][:], vef[i][:], exponent[:], ALU.pow).then_inc(sem(f"rsf_done{i}"), 1)

                    @block.vector
                    def _(dve):
                        with dve.Fori(0, BATCH // 2) as p:
                            for i in range(2):
                                for q in range(QS):
                                    last = nc.vector.bn_stats(stf[i][:, q, :], acc[:, bass.ds((p * 2 + i) * QS + q, 1), :].rearrange("p a d -> p (a d)"))
                                last.then_inc(sem(f"stf_done{i}"), 1)
                                dve.wait_ge(sem(f"stf_done{i}"), p + 1)
                                hold(dve)
                                for q in range(QS):
                                    last = nc.vector.bn_aggr(mvf[i][:, q, :], stf[i][:, q, :])
                                last.then_inc(sem(f"mvf_done{i}"), 1)
                                dve.wait_ge(sem(f"mvf_done{i}"), p + 1)
                                nc.vector.tensor_scalar(vef[i][:].unsqueeze(2), mvf[i][:, :, 1:2], LN_EPS, None, ALU.add).then_inc(sem(f"vef_done{i}"), 1)
                            for i in range(2):
                                dve.wait_ge(sem(f"rsf_done{i}"), p + 1)
                                for q in range(QS):
                                    last = nc.vector.tensor_scalar(normed[i][:, q, :], acc[:, bass.ds((p * 2 + i) * QS + q, 1), :].rearrange("p a d -> p (a d)"), mvf[i][:, q, 0:1], rsf[i][:, q:q + 1], ALU.subtract, ALU.mult)
                                last.then_inc(sem(f"normed_done{i}"), 1)
                                dve.wait_ge(sem(f"normed_done{i}"), p + 1)
                                dve.wait_ge(sem(f"x1_back{i}"), p * 16 + 16)
                                dve.wait_ge(sem(f"out_stored{i}"), p * 16)
                                nc.vector.tensor_tensor(final[i][:], normed[i][:], x1_in[i][:], ALU.add).then_inc(sem(f"final_done{i}"), 1)


_SHAPE_CONSTS = ("ident", "causal", "later", "index", "spread")


def _layout(inputs):
    def of(name):
        return np.asarray(inputs["L0_" + name])

    wide = ROUTED_CHUNKS * P
    routed = [np.transpose(of("ffn_w_" + n), (1, 0, 2)).reshape(D_MODEL, wide) for n in ("gate", "up")]
    pad = SHARED_CHUNKS * P - I_SHARED
    shared = [np.pad(of("ffn_sh_" + n), ((0, 0), (0, pad))) for n in ("gate", "up")]
    ups = [np.concatenate([r, s], axis=1).reshape(KD, P, CHUNKS, P) for r, s in zip(routed, shared)]
    down = np.concatenate([of("ffn_w_down").reshape(wide, D_MODEL),
                           np.pad(of("ffn_sh_down"), ((0, pad), (0, 0)))]).reshape(CHUNKS, P, D_MODEL)
    moe = np.concatenate([np.transpose(w, (2, 1, 0, 3)).reshape(CHUNKS, P, KD * P) for w in ups] + [down], axis=2)
    gates = np.concatenate([of("ffn_router_w").T, of("ffn_sh_gate_w")], axis=1)
    t = np.arange(P)
    causal = (t[:, None] <= t[None, :]).astype(np.float32)
    later = (t[:, None] > t[None, :]).astype(np.float32)
    unit = np.arange(CHUNKS * P)
    gate_of = np.minimum(unit // I_MOE, EXPERTS)
    one = (np.arange(GATES)[:, None] == gate_of[None, :]).astype(np.float32)
    spread = (np.tile(one, (PARTS, 1)).view(np.uint32) >> 16).astype(np.uint16).reshape(PARTS * GATES, CHUNKS, P)
    index = np.tile(np.arange(EXPERTS, dtype=np.float32), (P, 1))
    small = np.concatenate(
        [np.transpose(of("attn_conv_w").reshape(XBC_TILES, P, TAPS), (1, 0, 2)).reshape(P, -1),
         of("attn_conv_b").reshape(XBC_TILES, P).T, of("attn_norm_w").reshape(HEADS, P).T]
        + [np.tile(of("attn_" + n), (P, 1)) for n in ("dt_bias", "A_log", "D")], axis=1)
    return {**{"attn_" + n: of("attn_" + n) for n in ("u", "W_in", "W_out")}, "small": small, "gates": gates, "moe": moe,
            "ident": np.eye(P, dtype=np.float32), "causal": causal, "later": later, "index": index, "spread": spread}


def kernel(**inputs):
    import concourse.bacc as bacc
    from concourse.bass_utils import run_bass_kernel_spmd

    nc = bacc.Bacc("TRN2", target_bir_lowering=False, num_devices=1)
    arrays, args = {}, []
    for name, a in _layout(inputs).items():
        a = np.ascontiguousarray(a)
        arrays[f"in_{name}"] = a
        args.append(nc.dram_tensor(f"in_{name}", a.shape, mybir.dt.from_np(a.dtype), kind="ExternalInput").ap())
    args.append(nc.dram_tensor("out_0", (BATCH, SEQ, D_MODEL), mybir.dt.float32, kind="ExternalOutput").ap())
    sandwich_kernel(nc, *args)
    r = run_bass_kernel_spmd(nc, [arrays], core_ids=[0])
    return np.asarray(r.results[0]["out_0"])
```
